# Optimizing a Trainium2 kernel written in Bass

```python
import numpy as np
import jax
import jax.numpy as jnp

def _softmax(x, axis=-1):
    return jax.nn.softmax(x, axis=axis)

def _gelu(x):
    return jax.nn.gelu(x, approximate=True)

def _silu(x):
    return jax.nn.silu(x)

def _sigmoid(x):
    return jax.nn.sigmoid(x)

def _layernorm(x, axis=-1, eps=1e-05):
    m = jnp.mean(x, axis=axis, keepdims=True)
    v = jnp.var(x, axis=axis, keepdims=True)
    return (x - m) / jnp.sqrt(v + eps)

def _scatter_add(tgt, idx, src, axis=0):
    return tgt.at[idx].add(src)

def _segment_sum(src, seg, n):
    return jax.ops.segment_sum(src, seg, n)
kernel_name = 'mk_macaron_d1_jaxref_r8_d689f3'

def setup_inputs(seed: int=0):
    np.random.seed(seed)
    _w = jnp.asarray

    def _L0_attn_setup():
        import jax, jax.numpy as jnp
        import numpy as np
        THETA = 10000.0
        EPS = 1e-06
        N_HEADS = 16

        def apply_rope(x):
            b, h, l, d = x.shape
            inv_freq = 1.0 / THETA ** (jnp.arange(0, d, 2, dtype=jnp.float32) / d)
            t = jnp.arange(l, dtype=jnp.float32)
            freqs = t[:, None] * inv_freq[None, :]
            cos = jnp.cos(freqs)[None, None]
            sin = jnp.sin(freqs)[None, None]
            x1 = x[..., 0::2]
            x2 = x[..., 1::2]
            out = jnp.stack([x1 * cos - x2 * sin, x1 * sin + x2 * cos], axis=-1)
            return out.reshape(b, h, l, d)
        key = jax.random.key(seed)
        ks = jax.random.split(key, 5)
        dim = 128
        b, l = (1, 256)
        scale = 1.0 / np.sqrt(dim)
        return {'x': jax.random.normal(ks[0], (b, l, dim), dtype=jnp.float32), 'wq': jax.random.normal(ks[1], (dim, dim), dtype=jnp.float32) * scale, 'wk': jax.random.normal(ks[2], (dim, dim), dtype=jnp.float32) * scale, 'wv': jax.random.normal(ks[3], (dim, dim), dtype=jnp.float32) * scale, 'wo': jax.random.normal(ks[4], (dim, dim), dtype=jnp.float32) * scale}
    _L0_attn_in = _L0_attn_setup()

    def _L0_ffn_setup():
        import jax, jax.numpy as jnp
        import numpy as np
        D = 128
        H = 4
        DF = 512
        E = 8
        EPS = 1e-05

        def _layer_norm(x, g, b):
            mu = jnp.mean(x, axis=-1, keepdims=True)
            var = jnp.mean(jnp.square(x - mu), axis=-1, keepdims=True)
            return (x - mu) * jax.lax.rsqrt(var + EPS) * g + b

        def _mha(x, Wqkv, bqkv, Wo, bo):
            S, B, _ = x.shape
            hd = D // H
            qkv = x @ Wqkv.T + bqkv
            q, k, v = jnp.split(qkv, 3, axis=-1)
            to_heads = lambda t: t.reshape(S, B, H, hd).transpose(1, 2, 0, 3)
            q, k, v = (to_heads(q), to_heads(k), to_heads(v))
            scores = jnp.einsum('bhqd,bhkd->bhqk', q, k) * (1.0 / np.sqrt(hd))
            att = jax.nn.softmax(scores, axis=-1)
            o = jnp.einsum('bhqk,bhkd->bhqd', att, v)
            o = o.transpose(2, 0, 1, 3).reshape(S, B, D)
            return o @ Wo.T + bo

        def _moe(x, Wg, W1, b1, W2, b2):
            S, B, _ = x.shape
            xf = x.reshape(S * B, D)
            logits = xf @ Wg.T
            idx = jnp.argmax(logits, axis=-1)
            out = jnp.zeros_like(xf)
            for e in range(E):
                m = (idx == e)[:, None].astype(xf.dtype)
                h = jax.nn.relu(xf @ W1[e] + b1[e])
                out = out + m * (h @ W2[e] + b2[e])
            return out.reshape(S, B, D)
        key = jax.random.key(seed)
        ks = jax.random.split(key, 16)
        S, B = (64, 8)
        s = lambda k, shape, fan: jax.random.normal(k, shape, jnp.float32) * (1.0 / np.sqrt(fan))
        return {'x': jax.random.normal(ks[0], (S, B, D), jnp.float32), 'Wqkv': s(ks[1], (3 * D, D), D), 'bqkv': jnp.zeros((3 * D,), jnp.float32), 'Wo': s(ks[2], (D, D), D), 'bo': jnp.zeros((D,), jnp.float32), 'g1': jnp.ones((D,), jnp.float32), 'be1': jnp.zeros((D,), jnp.float32), 'g2': jnp.ones((D,), jnp.float32), 'be2': jnp.zeros((D,), jnp.float32), 'Wg': s(ks[3], (E, D), D), 'W1': s(ks[4], (E, D, DF), D), 'b1': jnp.zeros((E, DF), jnp.float32), 'W2': s(ks[5], (E, DF, D), DF), 'b2': jnp.zeros((E, D), jnp.float32)}
    _L0_ffn_in = _L0_ffn_setup()
    _d = {'L0_attn_x': _L0_attn_in['x'], 'L0_attn_wq': _L0_attn_in['wq'], 'L0_attn_wk': _L0_attn_in['wk'], 'L0_attn_wv': _L0_attn_in['wv'], 'L0_attn_wo': _L0_attn_in['wo'], 'L0_ffn_Wqkv': _L0_ffn_in['Wqkv'], 'L0_ffn_bqkv': _L0_ffn_in['bqkv'], 'L0_ffn_Wo': _L0_ffn_in['Wo'], 'L0_ffn_bo': _L0_ffn_in['bo'], 'L0_ffn_g1': _L0_ffn_in['g1'], 'L0_ffn_be1': _L0_ffn_in['be1'], 'L0_ffn_g2': _L0_ffn_in['g2'], 'L0_ffn_be2': _L0_ffn_in['be2'], 'L0_ffn_Wg': _L0_ffn_in['Wg'], 'L0_ffn_W1': _L0_ffn_in['W1'], 'L0_ffn_b1': _L0_ffn_in['b1'], 'L0_ffn_W2': _L0_ffn_in['W2'], 'L0_ffn_b2': _L0_ffn_in['b2']}
    _x0 = _d['L0_attn_x']
    _d['L0_attn_x'] = jax.random.normal(jax.random.fold_in(jax.random.key(seed), 1), (4, 1024, 128), dtype=_x0.dtype)
    del _x0
    return _d

def reference(L0_attn_x, L0_attn_wq, L0_attn_wk, L0_attn_wv, L0_attn_wo, L0_ffn_Wqkv, L0_ffn_bqkv, L0_ffn_Wo, L0_ffn_bo, L0_ffn_g1, L0_ffn_be1, L0_ffn_g2, L0_ffn_be2, L0_ffn_Wg, L0_ffn_W1, L0_ffn_b1, L0_ffn_W2, L0_ffn_b2):

    def _L0_attn_ref(x, wq, wk, wv, wo):
        import jax, jax.numpy as jnp
        import numpy as np
        THETA = 10000.0
        EPS = 1e-06
        N_HEADS = 16

        def apply_rope(x):
            b, h, l, d = x.shape
            inv_freq = 1.0 / THETA ** (jnp.arange(0, d, 2, dtype=jnp.float32) / d)
            t = jnp.arange(l, dtype=jnp.float32)
            freqs = t[:, None] * inv_freq[None, :]
            cos = jnp.cos(freqs)[None, None]
            sin = jnp.sin(freqs)[None, None]
            x1 = x[..., 0::2]
            x2 = x[..., 1::2]
            out = jnp.stack([x1 * cos - x2 * sin, x1 * sin + x2 * cos], axis=-1)
            return out.reshape(b, h, l, d)
        b, l, dim = x.shape
        h = N_HEADS
        d = dim // h
        q = (x @ wq).reshape(b, l, h, d)
        k = (x @ wk).reshape(b, l, h, d)
        v = (x @ wv).reshape(b, l, h, d)
        q = apply_rope(q.transpose(0, 2, 1, 3)).transpose(0, 2, 1, 3)
        k = apply_rope(k.transpose(0, 2, 1, 3)).transpose(0, 2, 1, 3)
        Q = jax.nn.relu(q)
        K = jax.nn.relu(k)
        kv_state = jnp.einsum('blhd,blhm->blhdm', K, v)
        kv_cumsum = jnp.cumsum(kv_state, axis=1)
        k_cumsum = jnp.cumsum(K, axis=1)
        numerator = jnp.einsum('blhd,blhdm->blhm', Q, kv_cumsum)
        denominator = jnp.einsum('blhd,blhd->blh', Q, k_cumsum)[..., None]
        out = numerator / (denominator + EPS)
        out = out.reshape(b, l, dim)
        return out @ wo

    def _L0_ffn_ref(x, Wqkv, bqkv, Wo, bo, g1, be1, g2, be2, Wg, W1, b1, W2, b2):
        import jax, jax.numpy as jnp
        import numpy as np
        D = 128
        H = 4
        DF = 512
        E = 8
        EPS = 1e-05

        def _layer_norm(x, g, b):
            mu = jnp.mean(x, axis=-1, keepdims=True)
            var = jnp.mean(jnp.square(x - mu), axis=-1, keepdims=True)
            return (x - mu) * jax.lax.rsqrt(var + EPS) * g + b

        def _mha(x, Wqkv, bqkv, Wo, bo):
            S, B, _ = x.shape
            hd = D // H
            qkv = x @ Wqkv.T + bqkv
            q, k, v = jnp.split(qkv, 3, axis=-1)
            to_heads = lambda t: t.reshape(S, B, H, hd).transpose(1, 2, 0, 3)
            q, k, v = (to_heads(q), to_heads(k), to_heads(v))
            scores = jnp.einsum('bhqd,bhkd->bhqk', q, k) * (1.0 / np.sqrt(hd))
            att = jax.nn.softmax(scores, axis=-1)
            o = jnp.einsum('bhqk,bhkd->bhqd', att, v)
            o = o.transpose(2, 0, 1, 3).reshape(S, B, D)
            return o @ Wo.T + bo

        def _moe(x, Wg, W1, b1, W2, b2):
            S, B, _ = x.shape
            xf = x.reshape(S * B, D)
            logits = xf @ Wg.T
            idx = jnp.argmax(logits, axis=-1)
            out = jnp.zeros_like(xf)
            for e in range(E):
                m = (idx == e)[:, None].astype(xf.dtype)
                h = jax.nn.relu(xf @ W1[e] + b1[e])
                out = out + m * (h @ W2[e] + b2[e])
            return out.reshape(S, B, D)
        y = _layer_norm(x + _mha(x, Wqkv, bqkv, Wo, bo), g1, be1)
        z = _layer_norm(y + _moe(y, Wg, W1, b1, W2, b2), g2, be2)
        return z
    x = L0_attn_x
    x = x + 0.5 * _L0_ffn_ref(_layernorm(x, axis=-1), L0_ffn_Wqkv, L0_ffn_bqkv, L0_ffn_Wo, L0_ffn_bo, L0_ffn_g1, L0_ffn_be1, L0_ffn_g2, L0_ffn_be2, L0_ffn_Wg, L0_ffn_W1, L0_ffn_b1, L0_ffn_W2, L0_ffn_b2)
    x = x + _L0_attn_ref(_layernorm(x, axis=-1), L0_attn_wq, L0_attn_wk, L0_attn_wv, L0_attn_wo)
    x = x + 0.5 * _L0_ffn_ref(_layernorm(x, axis=-1), L0_ffn_Wqkv, L0_ffn_bqkv, L0_ffn_Wo, L0_ffn_bo, L0_ffn_g1, L0_ffn_be1, L0_ffn_g2, L0_ffn_be2, L0_ffn_Wg, L0_ffn_W1, L0_ffn_b1, L0_ffn_W2, L0_ffn_b2)
    return x

_drawn_inputs = setup_inputs


def setup_inputs(seed=0):
    import zlib

    import numpy as np

    out = dict(_drawn_inputs(seed))
    spreads = {'L0_ffn_bqkv': (0.0, 0.1),
     'L0_ffn_bo': (0.0, 0.1),
     'L0_ffn_g1': (1.0, 0.2),
     'L0_ffn_be1': (0.0, 0.1),
     'L0_ffn_g2': (1.0, 0.2),
     'L0_ffn_be2': (0.0, 0.1),
     'L0_ffn_b1': (0.0, 0.1),
     'L0_ffn_b2': (0.0, 0.1)}
    factors = {}
    for name, (base, spread) in spreads.items():
        noise = np.random.default_rng([zlib.crc32(name.encode()), seed]).standard_normal(out[name].shape)
        drawn = base * np.exp(spread * noise) if base else spread * noise
        out[name] = jnp.asarray(drawn.astype(out[name].dtype))
    for name, factor in factors.items():
        out[name] = (out[name] * factor).astype(out[name].dtype)
    return out
```

```python
import concourse.bass as bass
from concourse import mybir
from contextlib import ExitStack

F32 = mybir.dt.float32
BF16 = mybir.dt.bfloat16
I32 = mybir.dt.int32
ALU = mybir.AluOpType
ACT = mybir.ActivationFunctionType
AX = mybir.AxisListType

P = 128
D = 128
S = 4
L = 1024
N = S * L
NJ = L // P
NT = N // P
H1, HD1 = 4, 32
H2, HD2 = 16, 8
HM = HD2 + 1
E, DF = 8, 512
NC = DF // P
SLOTS = NT + E
SPARE = SLOTS * P
EPS_LN, EPS_LA = 1e-5, 1e-6
PAIRS = S * S * H1

CONST_PARTS = [("ident", P), ("upto", P), ("before", P), ("ones", P), ("heads", H1), ("block", H2 * HM),
               ("lane", P), ("slot", SLOTS), ("filled", NT), ("rank", E), ("part", 1), ("spare", SLOTS),
               ("high", NT), ("cos", NJ * HD2), ("sin", NJ * HD2)]


def const_columns():
    at, where = 0, {}
    for name, width in CONST_PARTS:
        where[name] = (at, at + width)
        at += width
    return where, at


def after(engine, semaphore, count):
    if isinstance(count, int) and count <= 0:
        return
    engine.wait_ge(semaphore, count)


def apart(engine):
    engine.nop(nofuse=True)


def pipeline(engine, stages, count, unroll, first):
    depth = max(lag for _, lag in stages)
    loops = (count - first) // unroll

    def peeled(i):
        for stage, lag in stages:
            if 0 <= i - lag < count:
                stage(i - lag, (i - lag) % unroll, (i - lag) // unroll)

    for i in range(first):
        peeled(i)
    with engine.Fori(0, loops, 1) as turn:
        for k in range(unroll):
            for stage, lag in stages:
                at = first + k - lag
                stage(turn * unroll + at, at % unroll, turn + at // unroll)
    for i in range(first + loops * unroll, count + depth):
        peeled(i)


def bcast_mid(ap, n):
    return ap.unsqueeze(1).to_broadcast([ap.shape[0], n, ap.shape[1]])


def bcast_last(ap, n):
    return ap.unsqueeze(len(ap.shape)).to_broadcast(list(ap.shape) + [n])


class Names:

    def __init__(self, nc, ctx, phase, names):
        self.of = {}
        ctx.callback(self.clear, nc)
        for entry in names.split():
            name, _, k = entry.partition("*")
            for n in [f"{name}{b}" for b in range(int(k))] if k else [name]:
                self.of[n] = nc.alloc_semaphore(f"{phase}_{n}")

    def clear(self, nc):
        nc.clear_and_free_semaphores(list(self.of.values()))
        nc.all_engine_barrier()

    def __getitem__(self, name):
        return self.of[name]


def load_constants(nc, c, w, dram):
    with ExitStack() as ctx:
        sem = Names(nc, ctx, "load", "loaded")
        rows = [("bo", "bo"), ("g1", "g1"), ("be1", "be1"), ("g2", "g2"), ("be2", "be2")]
        LOADS = 10 + 1 + E + 1 + len(rows)
        block = ctx.enter_context(nc.Block())

        @block.sync
        def _(sp):
            sp.dma_start(w["const"][:, :], dram["const"]).then_inc(sem["loaded"], 16)
            sp.dma_start(w["wqkv"][:, :], dram["wqkv"]).then_inc(sem["loaded"], 16)
            sp.dma_start(w["wo"][:, :], dram["wo"]).then_inc(sem["loaded"], 16)
            sp.dma_start(w["wg"][:, :], dram["wg"]).then_inc(sem["loaded"], 16)
            sp.dma_start(w["bqkv"][:, :], dram["bqkv"]).then_inc(sem["loaded"], 16)
            sp.dma_start(w["b1"][:, :], dram["b1"]).then_inc(sem["loaded"], 16)
            for n, name in enumerate(["la_wq", "la_wk", "la_wv"]):
                sp.dma_start(w["la_wqkv"][:, n * D:(n + 1) * D], dram[name]).then_inc(sem["loaded"], 16)
            sp.dma_start(w["la_wo"][:, :], dram["la_wo"]).then_inc(sem["loaded"], 16)
            sp.wait_ge(sem["loaded"], 16 * LOADS)

        @block.scalar
        def _(act):
            act.dma_start(w["w1"][:, :].rearrange("p (e f) -> p e f", e=E),
                          dram["w1"].rearrange("e p f -> p e f")).then_inc(sem["loaded"], 16)
            for e in range(E):
                act.dma_start(w["w2"][:, e * DF:(e + 1) * DF].rearrange("p (k d) -> p k d", k=NC),
                              dram["w2"][e].rearrange("(k p) d -> p k d", p=P)).then_inc(sem["loaded"], 16)
            act.dma_start(w["b2"][:, :], dram["b2"].rearrange("e d -> (e d)").partition_broadcast(P))\
               .then_inc(sem["loaded"], 16)
            for name, source in rows:
                act.dma_start(w[name][:, :], dram[source].partition_broadcast(P)).then_inc(sem["loaded"], 16)

        @block.vector
        def _(dve):
            dve.memset(w["eps"][:, :], EPS_LN)
            dve.memset(w["state"][:, :], 0.0)
            for b in range(2):
                dve.memset(w["values"][b][:, :], 1.0)
            dve.wait_ge(sem["loaded"], 16 * LOADS)
            dve.tensor_copy(w["before16"][:, :], c["before"])
            dve.tensor_copy(w["ones16"][:, :], c["ones"])
            dve.tensor_scalar(w["g2h"][:, :], w["g2"][:, :], 0.5, None, ALU.mult)
            dve.tensor_scalar(w["be2h"][:, :], w["be2"][:, :], 0.5, None, ALU.mult)


def attention_phase(nc, c, w, dram, src, tag):
    SB = S * P
    with ExitStack() as ctx:
        def sb(name, shape, dt=F32):
            return ctx.enter_context(nc.sbuf_tensor(f"{tag}_{name}", shape, dt))

        def two(name, shape, dt=F32):
            return [sb(f"{name}_{b}", shape, dt) for b in range(2)]

        def bank(name):
            return ctx.enter_context(nc.psum_tensor(f"{tag}_{name}", [P, 512], F32))

        sem = Names(nc, ctx, tag, "x_loaded*2 yx_stored*2 stats moments std std1 rstd n nb nT nT_sb xb q k v q_sb k_sb v_sb "
                    "products scores top shifted exps sums inv att weighted oT oT_sb proj r stats1 moments1 "
                    "rstd1 z zg y yT yT_sb logits logits_sb top_done")
        x = two("x", [P, S, D])
        yx = two("yx", [P, S, 2 * D])
        n = two("n", [P, SB])
        nb = two("nb", [P, SB])
        nT = two("nT", [P, SB])
        qT = two("qT", [P, SB])
        kT = two("kT", [P, SB])
        v = two("v", [P, SB])
        prod = sb("prod", [P, S * S * P])
        weighted = sb("weighted", [P, S * S * P])
        oT = sb("oT", [P, SB])
        yT = sb("yT", [P, SB])
        res = sb("res", [P, SB])
        zg = sb("zg", [P, SB])
        stats, moments, rstd = two("stats", [P, S, 6]), two("moments", [P, S, 2]), two("rstd", [P, S])
        stats1, moments1, rstd1 = sb("stats1", [P, S, 6]), sb("moments1", [P, S, 2]), sb("rstd1", [P, S])
        std, std1 = sb("std", [P, S]), sb("std1", [P, S])
        top, shifted, exps = sb("top", [P, S * H1]), sb("shifted", [P, PAIRS]), sb("exps", [P, PAIRS])
        sums, inv, att = sb("sums", [P, S * H1]), sb("inv", [P, S * H1]), sb("att", [P, PAIRS])
        pT, pq, pk, pv, pS, pO, pW, pY = [bank(f"bank{i}") for i in range(8)]
        pL = pS[:, 128:128 + S * E]
        ident = c["ident"]
        src_v = src.rearrange("(s l) d -> l s d", s=S)
        yx_v = dram["yx"].rearrange("(s l) d -> l s d", s=S)
        block = ctx.enter_context(nc.Block())

        @block.sync
        def _(sp):
            def load(j, u, r):
                after(sp, sem["xb"], j - 1)
                sp.dma_start(x[u][:, :, :], src_v[bass.ds(j * P, P), :, :])\
                  .then_inc(sem[f"x_loaded{u}"], 16)

            def store(j, u, r):
                sp.wait_ge(sem["y"], j + 1)
                sp.wait_ge(sem["xb"], j + 1)
                sp.dma_start(yx_v[bass.ds(j * P, P), :, :], yx[u][:, :, :])\
                  .then_inc(sem[f"yx_stored{u}"], 16)

            pipeline(sp, [(store, 3), (load, 0)], NJ, 2, 4)
            for u in range(2):
                sp.wait_ge(sem[f"yx_stored{u}"], 16 * (NJ // 2))

        @block.gpsimd
        def _(pool):
            def with_bias(j, u, r):
                pool.wait_ge(sem["n"], S * (j + 1))
                after(pool, sem[f"yx_stored{u}"], 16 * r)
                pool.tensor_tensor(yx[u][:, :, D:2 * D], x[u][:, :, :], bcast_mid(w["be2h"][:, :], S), ALU.add)\
                    .then_inc(sem["xb"], 1)
                after(pool, sem["r"], j - 1)
                pool.tensor_tensor(nb[u][:, :].rearrange("p (s d) -> p s d", s=S),
                                   n[u][:, :].rearrange("p (s d) -> p s d", s=S),
                                   bcast_mid(w["bo"][:, :], S), ALU.add).then_inc(sem["nb"], 1)

            def affine(j, u, r):
                pool.wait_ge(sem["z"], S * (j + 1))
                pool.tensor_tensor(zg[:, :].rearrange("p (s d) -> p s d", s=S),
                                   res[:, :].rearrange("p (s d) -> p s d", s=S),
                                   bcast_mid(w["g1"][:, :], S), ALU.mult).then_inc(sem["zg"], 1)
                pool.wait_ge(sem["zg"], j + 1)
                pool.tensor_tensor(yx[u][:, :, 0:D], zg[:, :].rearrange("p (s d) -> p s d", s=S),
                                   bcast_mid(w["be1"][:, :], S), ALU.add).then_inc(sem["y"], 1)

            pipeline(pool, [(affine, 2), (with_bias, 0)], NJ, 2, 4)

        @block.vector
        def _(dve):
            def statistics(j, u, r):
                dve.wait_ge(sem[f"x_loaded{u}"], 16 * (r + 1))
                for s in range(S):
                    dve.bn_stats(stats[u][:, s, :], x[u][:, s, :]).then_inc(sem["stats"], 1)
                dve.wait_ge(sem["stats"], S * (j + 1))
                apart(dve)
                for s in range(S):
                    dve.bn_aggr(moments[u][:, s, :], stats[u][:, s, :]).then_inc(sem["moments"], 1)

            def normalise(j, u, r):
                dve.wait_ge(sem["std"], j + 1)
                after(dve, sem["n"], S * j)
                dve.reciprocal(rstd[u][:, :], std[:, :]).then_inc(sem["rstd"], 1)
                dve.wait_ge(sem["rstd"], j + 1)
                after(dve, sem["nT"], j - 1)
                after(dve, sem["nb"], j - 1)
                for s in range(S):
                    dve.tensor_scalar(n[u][:, s * D:(s + 1) * D], x[u][:, s, :], moments[u][:, s, 0:1],
                                      rstd[u][:, s:s + 1], ALU.subtract, ALU.mult).then_inc(sem["n"], 1)

            def products(j, u, r):
                dve.wait_ge(sem["q_sb"], j + 1)
                dve.wait_ge(sem["k_sb"], j + 1)
                after(dve, sem["scores"], j)
                for s in range(S):
                    dve.tensor_tensor(prod[:, s * SB:(s + 1) * SB].rearrange("p (t b) -> p t b", t=S),
                                      bcast_mid(qT[u][:, s * P:(s + 1) * P], S),
                                      kT[u][:, :].rearrange("p (t b) -> p t b", t=S), ALU.mult)\
                       .then_inc(sem["products"], 1)

            def shift(j, u, r):
                dve.wait_ge(sem["scores"], j + 1)
                by_t = pS[:, 0:PAIRS].rearrange("p (s t h) -> p s h t", s=S, t=S)
                dve.tensor_reduce(top[:, :].rearrange("p (s h) -> p s h", s=S), by_t, AX.X, ALU.max)\
                   .then_inc(sem["top"], 1)
                dve.wait_ge(sem["top"], j + 1)
                after(dve, sem["exps"], j)
                dve.tensor_tensor(shifted[:, :].rearrange("p (s t h) -> p s t h", s=S, t=S),
                                  pS[:, 0:PAIRS].rearrange("p (s t h) -> p s t h", s=S, t=S),
                                  top[:, :].rearrange("p (s h) -> p s h", s=S).unsqueeze(2)
                                  .to_broadcast([P, S, S, H1]), ALU.subtract).then_inc(sem["shifted"], 1)

            def weigh(j, u, r):
                dve.wait_ge(sem["exps"], j + 1)
                dve.tensor_reduce(sums[:, :].rearrange("p (s h) -> p s h", s=S),
                                  exps[:, :].rearrange("p (s t h) -> p s h t", s=S, t=S), AX.X, ALU.add)\
                   .then_inc(sem["sums"], 1)
                dve.wait_ge(sem["sums"], j + 1)
                dve.reciprocal(inv[:, :], sums[:, :]).then_inc(sem["inv"], 1)
                dve.wait_ge(sem["inv"], j + 1)
                dve.tensor_tensor(att[:, :].rearrange("p (s t h) -> p s t h", s=S, t=S),
                                  exps[:, :].rearrange("p (s t h) -> p s t h", s=S, t=S),
                                  inv[:, :].rearrange("p (s h) -> p s h", s=S).unsqueeze(2)
                                  .to_broadcast([P, S, S, H1]), ALU.mult).then_inc(sem["att"], 1)
                dve.wait_ge(sem["att"], j + 1)
                dve.wait_ge(sem["v_sb"], j + 1)
                after(dve, sem["oT"], j)
                for s in range(S):
                    dve.tensor_tensor(
                        weighted[:, s * SB:(s + 1) * SB].rearrange("p (g d) -> p g d", d=HD1),
                        bcast_last(att[:, s * S * H1:(s + 1) * S * H1], HD1),
                        v[u][:, :].rearrange("p (g d) -> p g d", d=HD1), ALU.mult).then_inc(sem["weighted"], 1)

            def residual(j, u, r):
                dve.wait_ge(sem["proj"], j + 1)
                dve.wait_ge(sem["nb"], j + 1)
                after(dve, sem["zg"], j)
                dve.tensor_tensor(res[:, :], pW[:, :], nb[u][:, :], ALU.add).then_inc(sem["r"], 1)
                dve.wait_ge(sem["r"], j + 1)
                for s in range(S):
                    dve.bn_stats(stats1[:, s, :], res[:, s * D:(s + 1) * D]).then_inc(sem["stats1"], 1)
                dve.wait_ge(sem["stats1"], S * (j + 1))
                apart(dve)
                for s in range(S):
                    dve.bn_aggr(moments1[:, s, :], stats1[:, s, :]).then_inc(sem["moments1"], 1)

            def centre(j, u, r):
                dve.wait_ge(sem["std1"], j + 1)
                after(dve, sem["z"], S * j)
                dve.reciprocal(rstd1[:, :], std1[:, :]).then_inc(sem["rstd1"], 1)
                dve.wait_ge(sem["rstd1"], j + 1)
                for s in range(S):
                    dve.tensor_scalar(res[:, s * D:(s + 1) * D], res[:, s * D:(s + 1) * D], moments1[:, s, 0:1],
                                      rstd1[:, s:s + 1], ALU.subtract, ALU.mult).then_inc(sem["z"], 1)

            def keep_logits(j, u, r):
                dve.wait_ge(sem["logits"], j + 1)
                dve.tensor_copy(w["logits"][:, bass.ds(j * S * E, S * E)], pL).then_inc(sem["logits_sb"], 1)

            pipeline(dve, [(products, 1), (residual, 2), (statistics, 0), (shift, 1), (centre, 2), (normalise, 0),
                           (weigh, 1), (keep_logits, 2)],
                     NJ, 2, 4)

        @block.scalar
        def _(act):
            def exponent(j, u, r):
                act.wait_ge(sem["shifted"], j + 1)
                after(act, sem["att"], j)
                act.activation(exps[:, :], shifted[:, :], ACT.Exp, scale=HD1 ** -0.5).then_inc(sem["exps"], 1)

            def deviation(j, u, r):
                act.wait_ge(sem["moments"], S * (j + 1))
                after(act, sem["rstd"], j)
                act.activation(std[:, :], moments[u][:, :, 1], ACT.Sqrt, bias=w["eps"][:, :]).then_inc(sem["std"], 1)

            def deviation1(j, u, r):
                act.wait_ge(sem["moments1"], S * (j + 1))
                after(act, sem["rstd1"], j)
                act.activation(std1[:, :], moments1[:, :, 1], ACT.Sqrt, bias=w["eps"][:, :]).then_inc(sem["std1"], 1)

            def project(j, u, r):
                act.wait_ge(sem["nT"], j + 1)
                after(act, sem["v"], j - 1)
                act.activation(nT[u][:, :], pT[:, :], ACT.Copy).then_inc(sem["nT_sb"], 1)
                act.wait_ge(sem["q"], j + 1)
                after(act, sem["products"], S * (j - 1))
                act.activation(qT[u][:, :], pq[:, :], ACT.Identity, bias=w["bqkv"][:, 0:1]).then_inc(sem["q_sb"], 1)
                act.wait_ge(sem["k"], j + 1)
                act.activation(kT[u][:, :], pk[:, :], ACT.Identity, bias=w["bqkv"][:, 1:2]).then_inc(sem["k_sb"], 1)
                act.wait_ge(sem["v"], j + 1)
                after(act, sem["weighted"], S * (j - 1))
                act.activation(v[u][:, :], pv[:, :], ACT.Copy).then_inc(sem["v_sb"], 1)

            def outputs(j, u, r):
                act.wait_ge(sem["oT"], j + 1)
                after(act, sem["proj"], j)
                act.activation(oT[:, :], pO[:, :], ACT.Identity, bias=w["bqkv"][:, 2:3]).then_inc(sem["oT_sb"], 1)

            def turned_y(j, u, r):
                act.wait_ge(sem["yT"], j + 1)
                after(act, sem["logits"], j)
                act.activation(yT[:, :], pY[:, :], ACT.Copy).then_inc(sem["yT_sb"], 1)

            pipeline(act, [(deviation1, 2), (deviation, 0), (exponent, 1), (project, 0), (outputs, 1), (turned_y, 2)],
                     NJ, 2, 4)

        @block.tensor
        def _(pe):
            def scores(j, u, r):
                after(pe, sem["shifted"], j)
                after(pe, sem["logits_sb"], j - 2)
                for s in range(S):
                    pe.wait_ge(sem["products"], S * j + s + 1)
                    for t in range(S):
                        g = s * S + t
                        last = pe.matmul(pS[:, g * H1:(g + 1) * H1], prod[:, g * P:(g + 1) * P], c["heads"],
                                         start=True, stop=True)
                last.then_inc(sem["scores"], 1)

            def project(j, u, r):
                pe.wait_ge(sem["n"], S * (j + 1))
                after(pe, sem["nT_sb"], j)
                for s in range(S):
                    last = pe.transpose(pT[:, s * P:(s + 1) * P], n[u][:, s * D:(s + 1) * D], ident)
                last.then_inc(sem["nT"], 1)
                pe.wait_ge(sem["nT_sb"], j + 1)
                after(pe, sem["q_sb"], j)
                pe.matmul(pq[:, :], w["wqkv"][:, 0:D], nT[u][:, :], start=True, stop=True).then_inc(sem["q"], 1)
                after(pe, sem["k_sb"], j)
                pe.matmul(pk[:, :], w["wqkv"][:, D:2 * D], nT[u][:, :], start=True, stop=True).then_inc(sem["k"], 1)
                after(pe, sem["v_sb"], j)
                for s in range(S):
                    last = pe.matmul(pv[:, s * D:(s + 1) * D], nT[u][:, s * P:(s + 1) * P],
                                     w["wqkv"][:, 2 * D:3 * D], start=True, stop=True)
                last.then_inc(sem["v"], 1)

            def attended(j, u, r):
                after(pe, sem["oT_sb"], j)
                for s in range(S):
                    pe.wait_ge(sem["weighted"], S * j + s + 1)
                    for t in range(S):
                        g = s * S + t
                        last = pe.matmul(pO[:, s * P:(s + 1) * P], weighted[:, g * P:(g + 1) * P], ident,
                                         start=(t == 0), stop=(t == S - 1))
                last.then_inc(sem["oT"], 1)
                pe.wait_ge(sem["oT_sb"], j + 1)
                after(pe, sem["r"], j)
                for s in range(S):
                    last = pe.matmul(pW[:, s * D:(s + 1) * D], oT[:, s * P:(s + 1) * P], w["wo"][:, :],
                                     start=True, stop=True)
                last.then_inc(sem["proj"], 1)

            def router(j, u, r):
                pe.wait_ge(sem["y"], j + 1)
                after(pe, sem["yT_sb"], j)
                for s in range(S):
                    last = pe.transpose(pY[:, s * P:(s + 1) * P], yx[u][:, s, 0:D], ident)
                last.then_inc(sem["yT"], 1)
                pe.wait_ge(sem["yT_sb"], j + 1)
                if isinstance(j, int) and j + 1 >= NJ:
                    pe.wait_ge(sem["shifted"], NJ)
                else:
                    pe.wait_ge(sem["shifted"], j + 2)
                after(pe, sem["logits_sb"], j)
                for s in range(S):
                    last = pe.matmul(pL[:, s * E:(s + 1) * E], yT[:, s * P:(s + 1) * P], w["wg"][:, :],
                                     start=True, stop=True)
                last.then_inc(sem["logits"], 1)

            pipeline(pe, [(scores, 1), (project, 0), (attended, 1), (router, 2)], NJ, 2, 4)


def routing_phase(nc, c, w, tag):
    EG = E * NT
    with ExitStack() as ctx:
        def sb(name, shape, dt=F32):
            return ctx.enter_context(nc.sbuf_tensor(f"{tag}_{name}", shape, dt))

        sem = Names(nc, ctx, tag, "dve prefix inverse")
        best, tied, first = sb("best", [P, NT]), sb("tied", [P, EG]), sb("first", [P, NT])
        chosen, chosen16 = sb("chosen", [P, EG]), sb("chosen16", [P, EG], BF16)
        totals, summed, zeros = sb("totals", [P, EG]), sb("summed", [P, EG]), sb("zeros", [P, EG])
        count, full, tiles = sb("count", [P, E]), sb("full", [P, EG]), sb("tiles", [P, E])
        ends, shift = sb("ends", [P, E]), sb("shift", [P, E])
        slot, where = sb("slot_of", [P, EG]), sb("where", [P, NT])
        where_i, tile_i, lane_i = sb("where_i", [P, NT], I32), sb("tile_i", [P, NT], I32), sb("lane_i", [P, NT], I32)
        tile_f, lane_f = sb("tile_f", [P, NT]), sb("lane_f", [P, NT])
        passed, expert = sb("passed", [P, SLOTS * (E - 1)]), sb("expert_f", [P, SLOTS])
        lanes = sb("lanes", [P, NT * P], BF16)
        marks = sb("marks", [P, NT * 3 * SLOTS], BF16)
        inverse, reads, empty = sb("inverse", [P, 3 * SLOTS]), sb("reads_f", [P, SLOTS]), sb("empty", [P, SLOTS])
        writes = sb("writes_f", [P, SLOTS])
        pR = ctx.enter_context(nc.psum_tensor(f"{tag}_pPrefix", [P, 512], F32))
        pI = ctx.enter_context(nc.psum_tensor(f"{tag}_pInverse", [P, 512], F32))
        by_e = "p (e g) -> p e g"
        count_at = {}
        marks_v = marks[:, :].rearrange("p (g k t) -> p g k t", g=NT, k=3)
        block = ctx.enter_context(nc.Block())

        @block.vector
        def _(dve):
            done = [0]

            def then(instruction):
                done[0] += 1
                instruction.then_inc(sem["dve"], 1)
                dve.wait_ge(sem["dve"], done[0])

            logits = w["logits"][:, :].rearrange("p (g e) -> p g e", e=E)
            tied_v = tied[:, :].rearrange("p (g e) -> p g e", e=E)
            dve.memset(zeros[:, :], 0.0)
            then(dve.tensor_reduce(best[:, :], logits, AX.X, ALU.max))
            then(dve.tensor_tensor(tied_v, logits, bcast_last(best[:, :], E), ALU.is_ge))
            then(dve.tensor_tensor(tied_v, tied_v, bcast_mid(c["rank"], NT), ALU.mult))
            then(dve.tensor_reduce(first[:, :], tied_v, AX.X, ALU.max))
            then(dve.tensor_tensor(chosen[:, :].rearrange("p (e g) -> p g e", e=E),
                                   bcast_mid(c["rank"], NT), bcast_last(first[:, :], E), ALU.is_equal))
            then(dve.tensor_copy(chosen16[:, :], chosen[:, :]))
            count_at["chosen"] = done[0]
            dve.wait_ge(sem["prefix"], 1)
            then(dve.tensor_copy(totals[:, :], pR[:, EG:2 * EG]))
            then(dve.tensor_tensor_scan(summed[:, :], totals[:, :], zeros[:, :], 0.0, ALU.add, ALU.add))
            then(dve.tensor_reduce(count[:, :], totals[:, :].rearrange(by_e, e=E), AX.X, ALU.add))
            then(dve.tensor_tensor(full[:, :].rearrange(by_e, e=E), bcast_last(count[:, :], NT),
                                   bcast_mid(c["filled"], E), ALU.is_gt))
            then(dve.tensor_reduce(tiles[:, :], full[:, :].rearrange(by_e, e=E), AX.X, ALU.add))
            then(dve.tensor_tensor_scan(ends[:, :], tiles[:, :], zeros[:, 0:E], 0.0, ALU.add, ALU.add))
            then(dve.tensor_tensor(summed[:, :], summed[:, :], totals[:, :], ALU.subtract))
            then(dve.tensor_tensor(shift[:, :], ends[:, :], tiles[:, :], ALU.subtract))
            then(dve.scalar_tensor_tensor(shift[:, :], shift[:, :], float(P),
                                          summed[:, :].rearrange(by_e, e=E)[:, :, 0], ALU.mult, ALU.subtract))
            then(dve.tensor_tensor(slot[:, :], summed[:, :], pR[:, 0:EG], ALU.add))
            then(dve.tensor_tensor(slot[:, :].rearrange(by_e, e=E), slot[:, :].rearrange(by_e, e=E),
                                   bcast_last(shift[:, :], NT), ALU.add))
            then(dve.tensor_tensor(slot[:, :], slot[:, :], chosen[:, :], ALU.mult))
            then(dve.tensor_reduce(where[:, :], slot[:, :].rearrange("p (e g) -> p g e", e=E), AX.X, ALU.add))
            then(dve.tensor_copy(where_i[:, :], where[:, :]))
            then(dve.tensor_scalar(tile_i[:, :], where_i[:, :], 7, None, ALU.logical_shift_right))
            then(dve.tensor_scalar(lane_i[:, :], where_i[:, :], P - 1, None, ALU.bitwise_and))
            then(dve.tensor_copy(tile_f[:, :], tile_i[:, :]))
            then(dve.tensor_copy(lane_f[:, :], lane_i[:, :]))
            then(dve.tensor_tensor(passed[:, :].rearrange("p (t e) -> p t e", e=E - 1), bcast_last(c["slot"], E - 1),
                                   bcast_mid(ends[:, 0:E - 1], SLOTS), ALU.is_ge))
            then(dve.tensor_reduce(expert[:, :], passed[:, :].rearrange("p (t e) -> p t e", e=E - 1), AX.X, ALU.add))
            then(dve.tensor_copy(w["expert"][:, :], expert[:, :]))
            then(dve.tensor_tensor(lanes[:, :].rearrange("p (g l) -> p g l", g=NT), bcast_mid(c["lane"], NT),
                                   bcast_last(lane_f[:, :], P), ALU.is_equal))
            then(dve.tensor_tensor(marks_v[:, :, 2, :], bcast_mid(c["slot"], NT), bcast_last(tile_f[:, :], SLOTS),
                                   ALU.is_equal))
            then(dve.tensor_scalar(marks_v[:, :, 0, :], marks_v[:, :, 2, :], c["part"], None, ALU.mult))
            then(dve.tensor_tensor(marks_v[:, :, 1, :], marks_v[:, :, 2, :], bcast_last(c["high"], SLOTS), ALU.mult))
            count_at["marks"] = done[0]
            dve.wait_ge(sem["inverse"], 1)
            then(dve.tensor_copy(inverse[:, :], pI[:, 0:3 * SLOTS]))
            low, high, used = [inverse[:, k * SLOTS:(k + 1) * SLOTS] for k in range(3)]
            then(dve.scalar_tensor_tensor(reads[:, :], high, float(P), low, ALU.mult, ALU.add))
            then(dve.tensor_scalar(empty[:, :], used, -1.0, 1.0, ALU.mult, ALU.add))
            then(dve.tensor_tensor(empty[:, :], empty[:, :], c["spare"], ALU.mult))
            then(dve.tensor_tensor(writes[:, :], reads[:, :], empty[:, :], ALU.add))
            then(dve.tensor_copy(w["reads"][:, :], reads[:, :]))
            then(dve.tensor_copy(w["writes"][:, :], writes[:, :]))

        @block.tensor
        def _(pe):
            pe.wait_ge(sem["dve"], count_at["chosen"])
            pe.matmul(pR[:, 0:EG], w["before16"][:, :], chosen16[:, :], start=True, stop=True)
            pe.matmul(pR[:, EG:2 * EG], w["ones16"][:, :], chosen16[:, :], start=True, stop=True)\
              .then_inc(sem["prefix"], 1)
            pe.wait_ge(sem["dve"], count_at["marks"])

            def locate(g, start, stop):
                return pe.matmul(pI[:, 0:3 * SLOTS], lanes[:, bass.ds(g * P, P)],
                                 marks[:, bass.ds(g * 3 * SLOTS, 3 * SLOTS)], start=start, stop=stop)

            locate(0, True, False)
            with pe.Fori(1, NT - 1, 1) as g:
                locate(g, False, False)
            locate(NT - 1, False, True).then_inc(sem["inverse"], 1)


def experts_phase(nc, c, w, dram, dst, tag):
    with ExitStack() as ctx:
        def sb(name, shape, dt=F32):
            return ctx.enter_context(nc.sbuf_tensor(f"{tag}_{name}", shape, dt))

        def some(k, name, shape, dt=F32):
            return [sb(f"{name}_{b}", shape, dt) for b in range(k)]

        def bank(name):
            return ctx.enter_context(nc.psum_tensor(f"{tag}_{name}", [P, 512], F32))

        sem = Names(nc, ctx, tag, "index gathered*4 w1 yT yT_sb h hb hT o a b stats moments std rstd zg out "
                    "out_index scattered*4")
        index, out_index = some(4, "index", [P, 1], I32), some(4, "out_index", [P, 1], I32)
        rows = some(4, "rows", [P, 2 * D])
        out = some(4, "out", [P, D])
        w1 = some(2, "w1", [P, DF])
        yT, hb, hT = some(2, "yT", [P, P]), some(2, "hb", [P, DF]), some(2, "hT", [P, DF])
        a, zg = sb("a", [P, D]), sb("zg", [P, D])
        stats, moments, rstd, std = sb("stats", [P, 6]), sb("moments", [P, 2]), sb("rstd", [P, 1]), sb("std", [P, 1])
        pT, pH, pO = bank("turn"), [bank("h0"), bank("h1")], [bank("o0"), bank("o1")]
        ident = c["ident"]
        block = ctx.enter_context(nc.Block())

        @block.gpsimd
        def _(pool):
            def gather(t, u, r):
                pool.wait_ge(sem["index"], t + 1)
                after(pool, sem["out"], t - 3)
                apart(pool)
                pool.indirect_dma_start(rows[u][:, :], None, dram["yx"],
                                        bass.IndirectOffsetOnAxis(ap=index[u][:, :], axis=0))\
                    .then_inc(sem[f"gathered{u}"], 16)

            def scatter(t, u, r):
                pool.wait_ge(sem["out_index"], t + 1)
                pool.wait_ge(sem["out"], t + 1)
                apart(pool)
                pool.indirect_dma_start(dst, bass.IndirectOffsetOnAxis(ap=out_index[u][:, :], axis=0),
                                        out[u][:, :], None).then_inc(sem[f"scattered{u}"], 16)

            pipeline(pool, [(gather, 0), (scatter, 4)], SLOTS, 4, 8)
            for u in range(4):
                pool.wait_ge(sem[f"scattered{u}"], 16 * (SLOTS // 4))

        @block.scalar
        def _(act):
            def weights(t, u, r):
                e = act.value_load(w["expert"][0:1, bass.ds(t, 1)], min_val=0, max_val=E - 1)
                after(act, sem["h"], t - 1)
                act.activation(w1[u % 2][:, :], w["w1"][:, bass.ds(e * DF, DF)], ACT.Copy).then_inc(sem["w1"], 1)

            def turned(t, u, r):
                act.wait_ge(sem["yT"], t + 1)
                after(act, sem["h"], t - 1)
                act.activation(yT[u % 2][:, :], pT[:, 0:P], ACT.Copy).then_inc(sem["yT_sb"], 1)

            def relu(t, u, r):
                act.wait_ge(sem["hb"], t + 1)
                after(act, sem["o"], t - 1)
                act.activation(hT[u % 2][:, :], hb[u % 2][:, :], ACT.Relu).then_inc(sem["hT"], 1)

            def deviation(t, u, r):
                act.wait_ge(sem["moments"], t + 1)
                after(act, sem["rstd"], t)
                act.activation(std[:, :], moments[:, 1:2], ACT.Sqrt, bias=w["eps"][:, :]).then_inc(sem["std"], 1)

            pipeline(act, [(weights, 1), (turned, 2), (deviation, 3), (relu, 2)], SLOTS, 4, 8)

        @block.tensor
        def _(pe):
            def turn(t, u, r):
                pe.wait_ge(sem[f"gathered{u}"], 16 * (r + 1))
                after(pe, sem["yT_sb"], t)
                pe.transpose(pT[:, 0:P], rows[u][:, 0:D], ident).then_inc(sem["yT"], 1)

            def up(t, u, r):
                pe.wait_ge(sem["w1"], t + 1)
                pe.wait_ge(sem["yT_sb"], t + 1)
                after(pe, sem["hb"], t - 1)
                for k in range(NC):
                    last = pe.matmul(pH[u % 2][:, k * P:(k + 1) * P], w1[u % 2][:, k * P:(k + 1) * P],
                                     yT[u % 2][:, :], start=True, stop=True)
                last.then_inc(sem["h"], 1)

            def down(t, u, r):
                e = pe.value_load(w["expert"][0:1, bass.ds(t, 1)], min_val=0, max_val=E - 1)
                pe.wait_ge(sem["hT"], t + 1)
                after(pe, sem["a"], t - 1)
                for k in range(NC):
                    last = pe.matmul(pO[u % 2][:, 0:D], hT[u % 2][:, k * P:(k + 1) * P],
                                     w["w2"][:, bass.ds(e * DF + k * D, D)], start=(k == 0), stop=(k == NC - 1))
                last.then_inc(sem["o"], 1)

            pipeline(pe, [(turn, 2), (down, 3), (up, 2)], SLOTS, 4, 8)

        @block.vector
        def _(dve):
            def bias(t, u, r):
                e = dve.value_load(w["expert"][0:1, bass.ds(t, 1)], min_val=0, max_val=E - 1)
                dve.wait_ge(sem["h"], t + 1)
                after(dve, sem["hT"], t - 1)
                dve.tensor_tensor(hb[u % 2][:, :].rearrange("p (k b) -> p k b", k=NC),
                                  pH[u % 2][:, :].rearrange("p (k b) -> p k b", k=NC),
                                  bcast_last(w["b1"][:, bass.ds(e * NC, NC)], P), ALU.add).then_inc(sem["hb"], 1)

            def indices(t, u, r):
                after(dve, sem[f"gathered{u}"], 16 * r)
                dve.tensor_copy(index[u][:, :], w["reads"][:, bass.ds(t, 1)]).then_inc(sem["index"], 1)

            def out_indices(t, u, r):
                after(dve, sem[f"scattered{u}"], 16 * r)
                dve.tensor_copy(out_index[u][:, :], w["writes"][:, bass.ds(t, 1)]).then_inc(sem["out_index"], 1)

            def statistics(t, u, r):
                e = dve.value_load(w["expert"][0:1, bass.ds(t, 1)], min_val=0, max_val=E - 1)
                dve.wait_ge(sem["o"], t + 1)
                dve.tensor_tensor(a[:, :], pO[u % 2][:, 0:D], w["b2"][:, bass.ds(e * D, D)], ALU.add)\
                   .then_inc(sem["b"], 1)
                dve.wait_ge(sem["b"], t + 1)
                dve.tensor_tensor(a[:, :], a[:, :], rows[u][:, 0:D], ALU.add).then_inc(sem["a"], 1)
                dve.wait_ge(sem["a"], t + 1)
                dve.bn_stats(stats[:, :], a[:, :]).then_inc(sem["stats"], 1)
                dve.wait_ge(sem["stats"], t + 1)
                apart(dve)
                dve.bn_aggr(moments[:, :], stats[:, :]).then_inc(sem["moments"], 1)
                dve.wait_ge(sem["moments"], t + 1)
                dve.scalar_tensor_tensor(zg[:, :], a[:, :], moments[:, 0:1], w["g2h"][:, :],
                                         ALU.subtract, ALU.mult).then_inc(sem["zg"], 1)

            def finish(t, u, r):
                dve.wait_ge(sem["std"], t + 1)
                dve.reciprocal(rstd[:, :], std[:, :]).then_inc(sem["rstd"], 1)
                dve.wait_ge(sem["rstd"], t + 1)
                dve.wait_ge(sem["zg"], t + 1)
                after(dve, sem[f"scattered{u}"], 16 * r)
                dve.scalar_tensor_tensor(out[u][:, :], zg[:, :], rstd[:, 0:1], rows[u][:, D:2 * D],
                                         ALU.mult, ALU.add).then_inc(sem["out"], 1)

            pipeline(dve, [(indices, 0), (statistics, 3), (bias, 2), (out_indices, 3), (finish, 3)], SLOTS, 4, 8)


def linear_attention_phase(nc, c, w, dram, src, dst, tag):
    QK = 2 * D
    KV = H2 * HM * HD2
    PIECES = [(0, 6), (6, 11), (11, 16)]
    with ExitStack() as ctx:
        def sb(name, shape, dt=F32):
            return ctx.enter_context(nc.sbuf_tensor(f"{tag}_{name}", shape, dt))

        def some(k, name, shape, dt=F32):
            return [sb(f"{name}_{b}", shape, dt) for b in range(k)]

        def bank(name):
            return ctx.enter_context(nc.psum_tensor(f"{tag}_{name}", [P, 512], F32))

        sem = Names(nc, ctx, tag, "x_loaded*4 stored*4 stats moments std rstd n nT nT_sb qkv qk_sb v_sb rc rs rot relu "
                    "QT QT_sb inc masked state inter kv cum prod num whole den inv o oT oT_sb proj out")
        x = some(4, "x", [P, D])
        n, out = some(2, "n", [P, D]), some(4, "out", [P, D])
        stats, moments, rstd, std = sb("stats", [P, 6]), sb("moments", [P, 2]), sb("rstd", [P, 1]), sb("std", [P, 1])
        nT = sb("nT", [P, P])
        qk, rc, rs, rot = sb("qk", [P, QK]), sb("rc", [P, QK]), sb("rs", [P, QK]), sb("rot", [P, QK])
        relu = some(2, "relu", [P, QK])
        values = w["values"]
        QT, masked = sb("QT", [P, P]), sb("masked", [P, H2 * HM])
        kv, prod = some(2, "kv", [P, KV]), sb("prod", [P, KV])
        num, den, inv = sb("num", [P, H2 * HM]), sb("den", [P, H2]), sb("inv", [P, H2])
        o, oT = sb("o", [P, D]), sb("oT", [P, P])
        pN, pQ, pT, pU, pI, pA, pB, pC = [bank(f"bank{i}") for i in range(8)]
        pieces = [pA, pB, pC]
        ident = c["ident"]
        hm = "p (h m) -> p h m"

        def state(u):
            return w["state"][:, u * H2 * HM:(u + 1) * H2 * HM]

        def row(t, u):
            return (t - u) * (P // S) + u * L

        block = ctx.enter_context(nc.Block())

        @block.sync
        def _(sp):
            def load(t, u, r):
                after(sp, sem["out"], t - 3)
                sp.dma_start(x[u][:, :], src[bass.ds(row(t, u), P), :]).then_inc(sem[f"x_loaded{u}"], 16)

            def store(t, u, r):
                sp.wait_ge(sem["out"], t + 1)
                sp.dma_start(dst[bass.ds(row(t, u), P), :], out[u][:, :]).then_inc(sem[f"stored{u}"], 16)

            pipeline(sp, [(load, 0), (store, 4)], NT, 4, 8)
            for u in range(4):
                sp.wait_ge(sem[f"stored{u}"], 16 * (NT // 4))

        @block.vector
        def _(dve):
            def statistics(t, u, r):
                dve.wait_ge(sem[f"x_loaded{u}"], 16 * (r + 1))
                dve.bn_stats(stats[:, :], x[u][:, :]).then_inc(sem["stats"], 1)
                dve.wait_ge(sem["stats"], t + 1)
                apart(dve)
                dve.bn_aggr(moments[:, :], stats[:, :]).then_inc(sem["moments"], 1)

            def normalise(t, u, r):
                dve.wait_ge(sem["std"], t + 1)
                dve.reciprocal(rstd[:, :], std[:, :]).then_inc(sem["rstd"], 1)
                dve.wait_ge(sem["rstd"], t + 1)
                after(dve, sem["nT"], t - 1)
                dve.tensor_scalar(n[u % 2][:, :], x[u][:, :], moments[:, 0:1], rstd[:, 0:1],
                                  ALU.subtract, ALU.mult).then_inc(sem["n"], 1)

            def mask(t, u, r):
                dve.wait_ge(sem["inc"], t + 1)
                after(dve, sem["state"], t)
                dve.tensor_tensor(masked[:, :], pU[:, 0:H2 * HM], c["block"], ALU.mult).then_inc(sem["masked"], 1)

            def attend(t, u, r):
                after(dve, sem["num"], t)
                for k, (h0, h1) in enumerate(PIECES):
                    dve.wait_ge(sem["cum"], 3 * t + k + 1)
                    q = relu[u % 2][:, h0 * HD2:h1 * HD2].rearrange("p (h d) -> p h d", d=HD2)
                    size = [P, h1 - h0, HM, HD2]
                    dve.tensor_tensor(
                        prod[:, h0 * HM * HD2:h1 * HM * HD2].rearrange("p (h m d) -> p h m d", m=HM, d=HD2),
                        pieces[k][:, 0:(h1 - h0) * HM * HD2].rearrange("p (h m d) -> p h m d", m=HM, d=HD2),
                        q.unsqueeze(2).to_broadcast(size), ALU.mult).then_inc(sem["prod"], 1)
                dve.wait_ge(sem["prod"], 3 * (t + 1))
                after(dve, sem["o"], t)
                dve.tensor_reduce(num[:, :], prod[:, :].rearrange("p (g d) -> p g d", d=HD2), AX.X, ALU.add)\
                   .then_inc(sem["num"], 1)
                dve.wait_ge(sem["num"], t + 1)
                dve.wait_ge(sem["inter"], t + 1)
                dve.tensor_tensor(num[:, :], num[:, :], pI[:, 0:H2 * HM], ALU.add).then_inc(sem["whole"], 1)
                dve.wait_ge(sem["whole"], t + 1)
                num_v = num[:, :].rearrange(hm, m=HM)
                dve.tensor_scalar(den[:, :], num_v[:, :, HD2], EPS_LA, None, ALU.add).then_inc(sem["den"], 1)
                dve.wait_ge(sem["den"], t + 1)
                dve.reciprocal(inv[:, :], den[:, :]).then_inc(sem["inv"], 1)
                dve.wait_ge(sem["inv"], t + 1)
                after(dve, sem["oT"], t)
                dve.tensor_tensor(o[:, :].rearrange("p (h m) -> p h m", m=HD2), num_v[:, :, 0:HD2],
                                  bcast_last(inv[:, :], HD2), ALU.mult).then_inc(sem["o"], 1)

            def finish(t, u, r):
                dve.wait_ge(sem["proj"], t + 1)
                after(dve, sem[f"stored{u}"], 16 * r)
                dve.tensor_tensor(out[u][:, :], pI[:, 256:256 + D], x[u][:, :], ALU.add)\
                   .then_inc(sem["out"], 1)

            pipeline(dve, [(statistics, 0), (mask, 2), (normalise, 0), (attend, 2), (finish, 3)], NT, 4, 8)

        @block.gpsimd
        def _(pool):
            def rotate(t, u, r):
                pool.wait_ge(sem["qk_sb"], t + 1)
                apart(pool)
                heads = [P, 2 * H2, HD2]
                cos = bcast_mid(c["cos"][:, bass.ds((t - u) * (HD2 // S), HD2)], 2 * H2)
                sin = c["sin"][:, bass.ds((t - u) * (HD2 // S), HD2)].rearrange("p (i two) -> p i two", two=2)
                pairs = "p (h i two) -> p h i two"
                pool.tensor_tensor(rc[:, :].rearrange("p (h d) -> p h d", d=HD2),
                                   qk[:, :].rearrange("p (h d) -> p h d", d=HD2), cos, ALU.mult)\
                    .then_inc(sem["rc"], 1)
                for side in range(2):
                    pool.tensor_tensor(rs[:, :].rearrange(pairs, i=HD2 // 2, two=2)[:, :, :, side],
                                       qk[:, :].rearrange(pairs, i=HD2 // 2, two=2)[:, :, :, 1 - side],
                                       bcast_mid(sin[:, :, side], 2 * H2), ALU.mult).then_inc(sem["rs"], 1)
                pool.wait_ge(sem["rc"], t + 1)
                pool.wait_ge(sem["rs"], 2 * (t + 1))
                after(pool, sem["relu"], t)
                pool.tensor_tensor(rot[:, :], rc[:, :], rs[:, :], ALU.add).then_inc(sem["rot"], 1)

            def outer(t, u, r):
                pool.wait_ge(sem["relu"], t + 1)
                pool.wait_ge(sem["v_sb"], t + 1)
                after(pool, sem["cum"], 3 * (t - 1))
                size = [P, H2, HM, HD2]
                k = relu[u % 2][:, D:QK].rearrange("p (h d) -> p h d", d=HD2)
                pool.tensor_tensor(kv[u % 2][:, :].rearrange("p (h m d) -> p h m d", m=HM, d=HD2),
                                   k.unsqueeze(2).to_broadcast(size),
                                   bcast_last(values[u % 2][:, :].rearrange(hm, m=HM), HD2), ALU.mult)\
                    .then_inc(sem["kv"], 1)

            def add_state(t, u, r):
                pool.wait_ge(sem["masked"], t + 1)
                pool.wait_ge(sem["inter"], t + 1)
                pool.tensor_tensor(state(u), state(u), masked[:, :], ALU.add).then_inc(sem["state"], 1)

            pipeline(pool, [(outer, 2), (add_state, 2), (rotate, 1)], NT, 4, 8)

        @block.scalar
        def _(act):
            def turned(t, u, r):
                act.wait_ge(sem["nT"], t + 1)
                after(act, sem["qkv"], t)
                act.activation(nT[:, :], pN[:, 0:P], ACT.Copy).then_inc(sem["nT_sb"], 1)

            def project(t, u, r):
                act.wait_ge(sem["qkv"], t + 1)
                after(act, sem["rc"], t)
                after(act, sem["rs"], 2 * t)
                act.activation(qk[:, :], pQ[:, 0:QK], ACT.Copy).then_inc(sem["qk_sb"], 1)
                after(act, sem["kv"], t - 1)
                after(act, sem["inc"], t - 1)
                act.activation(values[u % 2][:, :].rearrange(hm, m=HM)[:, :, 0:HD2],
                               pQ[:, QK:QK + D].rearrange("p (h m) -> p h m", m=HD2), ACT.Copy)\
                   .then_inc(sem["v_sb"], 1)

            def rectify(t, u, r):
                act.wait_ge(sem["rot"], t + 1)
                after(act, sem["kv"], t - 1)
                after(act, sem["inc"], t - 1)
                after(act, sem["QT"], t - 1)
                after(act, sem["prod"], 3 * (t - 1))
                act.activation(relu[u % 2][:, :], rot[:, :], ACT.Relu).then_inc(sem["relu"], 1)

            def queries(t, u, r):
                act.wait_ge(sem["QT"], t + 1)
                after(act, sem["inter"], t)
                act.activation(QT[:, :], pT[:, 0:P], ACT.Copy).then_inc(sem["QT_sb"], 1)

            def outputs(t, u, r):
                act.wait_ge(sem["oT"], t + 1)
                after(act, sem["proj"], t)
                act.activation(oT[:, :], pT[:, 0:P], ACT.Copy).then_inc(sem["oT_sb"], 1)

            def deviation(t, u, r):
                act.wait_ge(sem["moments"], t + 1)
                after(act, sem["rstd"], t)
                act.activation(std[:, :], moments[:, 1:2], ACT.Sqrt, bias=w["eps"][:, :]).then_inc(sem["std"], 1)

            pipeline(act, [(deviation, 0), (queries, 2), (turned, 1), (outputs, 3), (project, 1), (rectify, 1)], NT, 4, 8)

        @block.tensor
        def _(pe):
            def queries(t, u, r):
                pe.wait_ge(sem["relu"], t + 1)
                after(pe, sem["QT_sb"], t)
                after(pe, sem["oT_sb"], t - 1)
                pe.transpose(pT[:, 0:P], relu[u % 2][:, 0:D], ident).then_inc(sem["QT"], 1)

            def turn(t, u, r):
                pe.wait_ge(sem["n"], t + 1)
                after(pe, sem["nT_sb"], t)
                pe.transpose(pN[:, 0:P], n[u % 2][:, :], ident).then_inc(sem["nT"], 1)

            def increment(t, u, r):
                pe.wait_ge(sem["v_sb"], t + 1)
                after(pe, sem["masked"], t)
                pe.matmul(pU[:, 0:H2 * HM], relu[u % 2][:, D:QK], values[u % 2][:, :], start=True, stop=True)\
                  .then_inc(sem["inc"], 1)

            def running(t, u, r):
                pe.wait_ge(sem["kv"], t + 1)
                for k, (h0, h1) in enumerate(PIECES):
                    after(pe, sem["prod"], 3 * (t - 1) + k + 1)
                    pe.matmul(pieces[k][:, 0:(h1 - h0) * HM * HD2], c["upto"],
                              kv[u % 2][:, h0 * HM * HD2:h1 * HM * HD2], start=True, stop=True)\
                      .then_inc(sem["cum"], 1)

            def earlier(t, u, r):
                pe.wait_ge(sem["QT_sb"], t + 1)
                after(pe, sem["state"], t - S + 1)
                after(pe, sem["whole"], t)
                after(pe, sem["out"], t - 1)
                pe.matmul(pI[:, 0:H2 * HM], QT[:, :], state(u), start=True, stop=True).then_inc(sem["inter"], 1)

            def project(t, u, r):
                pe.wait_ge(sem["nT_sb"], t + 1)
                after(pe, sem["v_sb"], t)
                pe.matmul(pQ[:, 0:3 * D], nT[:, :], w["la_wqkv"][:, :], start=True, stop=True)\
                  .then_inc(sem["qkv"], 1)

            def output(t, u, r):
                pe.wait_ge(sem["o"], t + 1)
                if isinstance(t, int) and t + 1 >= NT:
                    pe.wait_ge(sem["QT_sb"], NT)
                else:
                    pe.wait_ge(sem["QT_sb"], t + 2)
                pe.transpose(pT[:, 0:P], o[:, :], ident).then_inc(sem["oT"], 1)

            def combine(t, u, r):
                pe.wait_ge(sem["oT_sb"], t + 1)
                if isinstance(t, int) and t + 1 >= NT:
                    pe.wait_ge(sem["whole"], NT)
                else:
                    pe.wait_ge(sem["whole"], t + 2)
                after(pe, sem["out"], t)
                pe.matmul(pI[:, 256:256 + D], oT[:, :], w["la_wo"][:, :], start=True, stop=True)\
                  .then_inc(sem["proj"], 1)

            pipeline(pe, [(queries, 2), (turn, 1), (increment, 2), (earlier, 2), (output, 3), (project, 1),
                          (running, 2), (combine, 3)], NT, 4, 8)


def copy_out(nc, dram, out):
    with ExitStack() as ctx:
        copied = ctx.enter_context(nc.semaphore("copied"))
        block = ctx.enter_context(nc.Block())

        @block.sync
        def _(sp):
            sp.dma_start(out.rearrange("s l d -> (s l) d"), dram["x3"][0:N, :]).then_inc(copied, 16)
            sp.wait_ge(copied, 16)


def macaron_kernel(nc, dram, out):
    where, width = const_columns()
    with ExitStack() as ctx:
        def sb(name, shape, dt=F32):
            return ctx.enter_context(nc.sbuf_tensor(f"w_{name}", shape, dt))

        w = {name: sb(name, shape) for name, shape in [
            ("const", [P, width]), ("wqkv", [P, 3 * D]), ("wo", [P, D]), ("wg", [P, E]), ("bqkv", [P, 3]),
            ("w1", [P, E * DF]), ("w2", [P, E * DF]), ("b1", [P, E * NC]), ("b2", [P, E * D]),
            ("la_wqkv", [P, 3 * D]), ("la_wo", [P, D]), ("bo", [P, D]), ("g1", [P, D]), ("be1", [P, D]),
            ("g2", [P, D]), ("be2", [P, D]), ("g2h", [P, D]), ("be2h", [P, D]), 
            ("eps", [P, 1]), ("state", [P, S * H2 * HM]), ("logits", [P, NT * E])]}
        w["before16"], w["ones16"] = sb("before16", [P, P], BF16), sb("ones16", [P, P], BF16)
        for name in ["expert", "reads", "writes"]:
            w[name] = sb(name, [P, SLOTS], I32)
        w["values"] = [sb(f"values{b}", [P, H2 * HM]) for b in range(2)]
        c = {name: w["const"][:, a:b] for name, (a, b) in where.items()}
        dram["yx"] = nc.dram_tensor("rows_yx", [N, 2 * D], F32, kind="Internal").ap()
        dram["x1"] = nc.dram_tensor("rows_x1", [N + SPARE, D], F32, kind="Internal").ap()
        dram["x2"] = nc.dram_tensor("rows_x2", [N, D], F32, kind="Internal").ap()
        dram["x3"] = nc.dram_tensor("rows_x3", [N + SPARE, D], F32, kind="Internal").ap()
        load_constants(nc, c, w, dram)
        attention_phase(nc, c, w, dram, dram["x"], "a1")
        routing_phase(nc, c, w, "r1")
        experts_phase(nc, c, w, dram, dram["x1"], "e1")
        linear_attention_phase(nc, c, w, dram, dram["x1"], dram["x2"], "la")
        attention_phase(nc, c, w, dram, dram["x2"], "a2")
        routing_phase(nc, c, w, "r2")
        experts_phase(nc, c, w, dram, dram["x3"], "e2")
        copy_out(nc, dram, out)


def shape_constants():
    import numpy as np
    where, width = const_columns()
    table = np.zeros((P, width), np.float32)

    def put(name, a):
        table[:, where[name][0]:where[name][1]] = a

    i = np.arange(P)
    put("ident", np.eye(P))
    put("upto", i[:, None] <= i[None, :])
    put("before", i[:, None] < i[None, :])
    put("ones", 1.0)
    put("heads", i[:, None] // HD1 == np.arange(H1)[None, :])
    put("block", i[:, None] // HD2 == (np.arange(H2 * HM) // HM)[None, :])
    put("lane", i[None, :])
    put("slot", np.arange(SLOTS)[None, :])
    put("filled", (P * np.arange(NT))[None, :])
    put("rank", (E - np.arange(E))[None, :])
    put("part", i[:, None])
    put("spare", N + i[:, None] + P * np.arange(SLOTS)[None, :])
    g = np.arange(NT)
    put("high", ((g % S) * NJ + g // S)[None, :])
    inv_freq = (np.float32(1.0) / np.power(np.float32(10000.0), np.arange(0, HD2, 2, dtype=np.float32) / np.float32(HD2))).astype(np.float32)
    freqs = np.arange(L, dtype=np.float32)[:, None] * inv_freq[None, :]
    cos = np.cos(freqs.astype(np.float64)).astype(np.float32)
    sin = np.sin(freqs.astype(np.float64)).astype(np.float32)
    cos2 = np.repeat(cos, 2, axis=1)
    sin2 = np.stack([-sin, sin], axis=2).reshape(L, HD2)
    put("cos", cos2.reshape(NJ, P, HD2).transpose(1, 0, 2).reshape(P, NJ * HD2))
    put("sin", sin2.reshape(NJ, P, HD2).transpose(1, 0, 2).reshape(P, NJ * HD2))
    return table


def kernel(**inputs):
    import numpy as np
    import concourse.bacc as bacc
    from concourse.bass_utils import run_bass_kernel_spmd

    def lay(name):
        return np.asarray(inputs[name])

    arrays = {
        "x": lay("L0_attn_x").reshape(N, D),
        "wqkv": lay("L0_ffn_Wqkv").T, "wo": lay("L0_ffn_Wo").T, "wg": lay("L0_ffn_Wg").T,
        "bqkv": lay("L0_ffn_bqkv").reshape(3, D).T, "w1": lay("L0_ffn_W1"), "w2": lay("L0_ffn_W2"),
        "b1": lay("L0_ffn_b1").reshape(E * NC, P).T, "b2": lay("L0_ffn_b2"), "bo": lay("L0_ffn_bo"),
        "g1": lay("L0_ffn_g1"), "be1": lay("L0_ffn_be1"), "g2": lay("L0_ffn_g2"), "be2": lay("L0_ffn_be2"),
        "la_wq": lay("L0_attn_wq"), "la_wk": lay("L0_attn_wk"), "la_wv": lay("L0_attn_wv"),
        "la_wo": lay("L0_attn_wo"), "const": shape_constants(),
    }
    nc = bacc.Bacc("TRN2", target_bir_lowering=False, num_devices=1)
    sent, dram = {}, {}
    for name, a in arrays.items():
        sent[f"in_{name}"] = np.ascontiguousarray(a)
        dram[name] = nc.dram_tensor(f"in_{name}", list(a.shape), F32, kind="ExternalInput").ap()
    out = nc.dram_tensor("out", [S, L, D], F32, kind="ExternalOutput").ap()
    macaron_kernel(nc, dram, out)
    r = run_bass_kernel_spmd(nc, [sent], core_ids=[0])
    return r.results[0]["out"]
```

```python
import concourse.bass as bass
from concourse import mybir
from contextlib import ExitStack

F32 = mybir.dt.float32
BF16 = mybir.dt.bfloat16
I32 = mybir.dt.int32
ALU = mybir.AluOpType
ACT = mybir.ActivationFunctionType
AX = mybir.AxisListType

P = 128
D = 128
S = 4
L = 1024
N = S * L
NJ = L // P
NT = N // P
H1, HD1 = 4, 32
H2, HD2 = 16, 8
HM = HD2 + 1
E, DF = 8, 512
NC = DF // P
SLOTS = NT + E
SPARE = SLOTS * P
EPS_LN, EPS_LA = 1e-5, 1e-6
PAIRS = S * S * H1

CONST_PARTS = [("ident", P), ("upto", P), ("before", P), ("later", P), ("ones", P), ("heads", H1),
               ("lane", P), ("slot", SLOTS), ("filled", NT), ("rank", E), ("part", 1), ("spare", SLOTS),
               ("high", NT), ("cos", NJ * HD2), ("sin", NJ * HD2)]


def const_columns():
    at, where = 0, {}
    for name, width in CONST_PARTS:
        where[name] = (at, at + width)
        at += width
    return where, at


def after(engine, semaphore, count):
    if isinstance(count, int) and count <= 0:
        return
    engine.wait_ge(semaphore, count)


def apart(engine):
    engine.nop(nofuse=True)


def pipeline(engine, stages, count, unroll, first, experts=None):
    depth = max(lag for _, lag in stages)
    loops = (count - first) // unroll

    def load(i, n):
        if experts:
            experts.load(i, n)

    def peeled(i):
        if experts:
            experts.step += 1
        for stage, lag in stages:
            if 0 <= i - lag < count:
                stage(i - lag, (i - lag) % unroll, (i - lag) // unroll)

    load(0, first)
    for i in range(first):
        peeled(i)
    with engine.Fori(0, loops, 1) as turn:
        load(turn * unroll + first, unroll)
        for k in range(unroll):
            if experts:
                experts.step += 1
            for stage, lag in stages:
                at = first + k - lag
                stage(turn * unroll + at, at % unroll, turn + at // unroll)
    load(first + loops * unroll, count + depth - first - loops * unroll)
    for i in range(first + loops * unroll, count + depth):
        peeled(i)


def bcast_mid(ap, n):
    return ap.unsqueeze(1).to_broadcast([ap.shape[0], n, ap.shape[1]])


def bcast_last(ap, n):
    return ap.unsqueeze(len(ap.shape)).to_broadcast(list(ap.shape) + [n])


class Experts:

    def __init__(self, nc, w, engine, lags):
        self.nc, self.w, self.engine, self.lags = nc, w, engine, lags

    def load(self, i, n):
        lo, hi = i - max(self.lags), i + n - min(self.lags)
        if isinstance(i, int):
            lo, hi = max(lo, 0), min(hi, SLOTS)
            count = hi - lo
        else:
            count = n + max(self.lags) - min(self.lags)
        _, self.values = self.nc.values_load_multi_w_load_instructions(
            self.w["expert"][0:1, bass.ds(lo, count)], engines=[self.engine], min_val=0, max_val=E - 1)
        self.skipped = lo - (i - max(self.lags)) if isinstance(i, int) else 0
        self.step = -1

    def of(self, lag):
        return self.values[self.step + max(self.lags) - lag - self.skipped]


class Names:

    def __init__(self, nc, ctx, phase, names):
        self.of = {}
        ctx.callback(self.clear, nc)
        for entry in names.split():
            name, _, k = entry.partition("*")
            for n in [f"{name}{b}" for b in range(int(k))] if k else [name]:
                self.of[n] = nc.alloc_semaphore(f"{phase}_{n}")

    def clear(self, nc):
        nc.clear_and_free_semaphores(list(self.of.values()))
        nc.all_engine_barrier()

    def __getitem__(self, name):
        return self.of[name]


def load_constants(nc, c, w, dram):
    with ExitStack() as ctx:
        sem = Names(nc, ctx, "load", "loaded")
        rows = [("bo", "bo"), ("g1", "g1"), ("be1", "be1"), ("g2", "g2"), ("be2", "be2")]
        LOADS = 10 + 1 + E + 1 + len(rows)
        block = ctx.enter_context(nc.Block())

        @block.sync
        def _(sp):
            sp.dma_start(w["const"][:, :], dram["const"]).then_inc(sem["loaded"], 16)
            sp.dma_start(w["wqkv"][:, :], dram["wqkv"]).then_inc(sem["loaded"], 16)
            sp.dma_start(w["wo"][:, :], dram["wo"]).then_inc(sem["loaded"], 16)
            sp.dma_start(w["wg"][:, :], dram["wg"]).then_inc(sem["loaded"], 16)
            sp.dma_start(w["bqkv"][:, :], dram["bqkv"]).then_inc(sem["loaded"], 16)
            sp.dma_start(w["b1"][:, :], dram["b1"]).then_inc(sem["loaded"], 16)
            for n, name in enumerate(["la_wq", "la_wk", "la_wv"]):
                sp.dma_start(w["la_wqkv"][:, n * D:(n + 1) * D], dram[name]).then_inc(sem["loaded"], 16)
            sp.dma_start(w["la_wo"][:, :], dram["la_wo"]).then_inc(sem["loaded"], 16)
            sp.wait_ge(sem["loaded"], 16 * LOADS)

        @block.scalar
        def _(act):
            act.dma_start(w["w1"][:, :].rearrange("p (e f) -> p e f", e=E),
                          dram["w1"].rearrange("e p f -> p e f")).then_inc(sem["loaded"], 16)
            for e in range(E):
                act.dma_start(w["w2"][:, e * DF:(e + 1) * DF].rearrange("p (k d) -> p k d", k=NC),
                              dram["w2"][e].rearrange("(k p) d -> p k d", p=P)).then_inc(sem["loaded"], 16)
            act.dma_start(w["b2"][:, :], dram["b2"].rearrange("e d -> (e d)").partition_broadcast(P))\
               .then_inc(sem["loaded"], 16)
            for name, source in rows:
                act.dma_start(w[name][:, :], dram[source].partition_broadcast(P)).then_inc(sem["loaded"], 16)

        @block.vector
        def _(dve):
            dve.memset(w["eps"][:, :], EPS_LN)
            for b in range(4):
                dve.memset(w["values"][b][:, :], 1.0)
            dve.wait_ge(sem["loaded"], 16 * LOADS)
            dve.tensor_copy(w["before16"][:, :], c["before"])
            dve.tensor_copy(w["ones16"][:, :], c["ones"])
            dve.tensor_scalar(w["g2h"][:, :], w["g2"][:, :], 0.5, None, ALU.mult)
            dve.tensor_scalar(w["be2h"][:, :], w["be2"][:, :], 0.5, None, ALU.mult)


def attention_phase(nc, c, w, dram, tag, load_x):
    SB = S * P
    with ExitStack() as ctx:
        def sb(name, shape, dt=F32):
            return ctx.enter_context(nc.sbuf_tensor(f"{tag}_{name}", shape, dt))

        def two(name, shape, dt=F32):
            return [sb(f"{name}_{b}", shape, dt) for b in range(2)]

        def bank(name):
            return ctx.enter_context(nc.psum_tensor(f"{tag}_{name}", [P, 512], F32))

        sem = Names(nc, ctx, tag, "x_loaded yx_stored*2 stats moments std std1 rstd n nb nT nT_sb xb q k v q_sb k_sb v_sb "
                    "products scores top shifted exps sums inv att weighted oT oT_sb proj r stats1 moments1 "
                    "rstd1 z zg y yT yT_sb logits logits_sb top_done")
        x_all = w["x"][:, :].rearrange("p (s j d) -> p s j d", s=S, d=D)

        def x(j):
            return x_all[:, :, bass.ds(j, 1), :].rearrange("p s one d -> p s (one d)")

        yx = two("yx", [P, S, 2 * D])
        n = two("n", [P, SB])
        nb = two("nb", [P, SB])
        nT = two("nT", [P, SB])
        qT = two("qT", [P, SB])
        kT = two("kT", [P, SB])
        v = two("v", [P, SB])
        prod = sb("prod", [P, S * S * P])
        weighted = sb("weighted", [P, S * S * P])
        oT = sb("oT", [P, SB])
        yT = sb("yT", [P, SB])
        res = sb("res", [P, SB])
        zg = sb("zg", [P, SB])
        stats, moments, rstd = two("stats", [P, S, 6]), two("moments", [P, S, 2]), two("rstd", [P, S])
        stats1, moments1, rstd1 = sb("stats1", [P, S, 6]), sb("moments1", [P, S, 2]), sb("rstd1", [P, S])
        std, std1 = sb("std", [P, S]), sb("std1", [P, S])
        top, shifted, exps = sb("top", [P, S * H1]), sb("shifted", [P, PAIRS]), sb("exps", [P, PAIRS])
        sums, inv, att = sb("sums", [P, S * H1]), sb("inv", [P, S * H1]), sb("att", [P, PAIRS])
        pT, pq, pk, pv, pS, pO, pW, pY = [bank(f"bank{i}") for i in range(8)]
        pL = pS[:, 128:128 + S * E]
        ident = c["ident"]
        src_v = dram["x"].rearrange("(s l) d -> l s d", s=S)
        yx_v = dram["yx"].rearrange("(s l) d -> l s d", s=S)
        block = ctx.enter_context(nc.Block())

        @block.sync
        def _(sp):
            if load_x:
                for j in range(NJ):
                    sp.dma_start(x_all[:, :, j, :], src_v[j * P:(j + 1) * P, :, :]).then_inc(sem["x_loaded"], 16)
                    sp.wait_ge(sem["x_loaded"], 16 * (j + 1))

            def store(j, u, r):
                sp.wait_ge(sem["y"], j + 1)
                sp.wait_ge(sem["xb"], j + 1)
                sp.dma_start(yx_v[bass.ds(j * P, P), :, :], yx[u][:, :, :])\
                  .then_inc(sem[f"yx_stored{u}"], 16)

            pipeline(sp, [(store, 3)], NJ, 2, 4)
            for u in range(2):
                sp.wait_ge(sem[f"yx_stored{u}"], 16 * (NJ // 2))

        @block.gpsimd
        def _(pool):
            def with_bias(j, u, r):
                pool.wait_ge(sem["n"], S * (j + 1))
                after(pool, sem[f"yx_stored{u}"], 16 * r)
                apart(pool)
                pool.tensor_tensor(yx[u][:, :, D:2 * D], x(j), bcast_mid(w["be2h"][:, :], S), ALU.add)\
                    .then_inc(sem["xb"], 1)
                after(pool, sem["r"], j - 1)
                pool.tensor_tensor(nb[u][:, :].rearrange("p (s d) -> p s d", s=S),
                                   n[u][:, :].rearrange("p (s d) -> p s d", s=S),
                                   bcast_mid(w["bo"][:, :], S), ALU.add).then_inc(sem["nb"], 1)

            def affine(j, u, r):
                pool.wait_ge(sem["z"], S * (j + 1))
                pool.tensor_tensor(zg[:, :].rearrange("p (s d) -> p s d", s=S),
                                   res[:, :].rearrange("p (s d) -> p s d", s=S),
                                   bcast_mid(w["g1"][:, :], S), ALU.mult).then_inc(sem["zg"], 1)
                pool.wait_ge(sem["zg"], j + 1)
                pool.tensor_tensor(yx[u][:, :, 0:D], zg[:, :].rearrange("p (s d) -> p s d", s=S),
                                   bcast_mid(w["be1"][:, :], S), ALU.add).then_inc(sem["y"], 1)

            pipeline(pool, [(affine, 2), (with_bias, 0)], NJ, 2, 4)

        @block.vector
        def _(dve):
            def statistics(j, u, r):
                if load_x:
                    dve.wait_ge(sem["x_loaded"], 16 * (j + 1))
                    apart(dve)
                for s in range(S):
                    dve.bn_stats(stats[u][:, s, :], x(j)[:, s, :]).then_inc(sem["stats"], 1)
                dve.wait_ge(sem["stats"], S * (j + 1))
                apart(dve)
                for s in range(S):
                    dve.bn_aggr(moments[u][:, s, :], stats[u][:, s, :]).then_inc(sem["moments"], 1)

            def normalise(j, u, r):
                dve.wait_ge(sem["std"], j + 1)
                after(dve, sem["n"], S * j)
                dve.reciprocal(rstd[u][:, :], std[:, :]).then_inc(sem["rstd"], 1)
                dve.wait_ge(sem["rstd"], j + 1)
                after(dve, sem["nT"], j - 1)
                after(dve, sem["nb"], j - 1)
                for s in range(S):
                    dve.tensor_scalar(n[u][:, s * D:(s + 1) * D], x(j)[:, s, :], moments[u][:, s, 0:1],
                                      rstd[u][:, s:s + 1], ALU.subtract, ALU.mult).then_inc(sem["n"], 1)

            def products(j, u, r):
                dve.wait_ge(sem["q_sb"], j + 1)
                dve.wait_ge(sem["k_sb"], j + 1)
                after(dve, sem["scores"], j)
                for s in range(S):
                    dve.tensor_tensor(prod[:, s * SB:(s + 1) * SB].rearrange("p (t b) -> p t b", t=S),
                                      bcast_mid(qT[u][:, s * P:(s + 1) * P], S),
                                      kT[u][:, :].rearrange("p (t b) -> p t b", t=S), ALU.mult)\
                       .then_inc(sem["products"], 1)

            def shift(j, u, r):
                dve.wait_ge(sem["scores"], j + 1)
                by_t = pS[:, 0:PAIRS].rearrange("p (s t h) -> p s h t", s=S, t=S)
                dve.tensor_reduce(top[:, :].rearrange("p (s h) -> p s h", s=S), by_t, AX.X, ALU.max)\
                   .then_inc(sem["top"], 1)
                dve.wait_ge(sem["top"], j + 1)
                after(dve, sem["exps"], j)
                dve.tensor_tensor(shifted[:, :].rearrange("p (s t h) -> p s t h", s=S, t=S),
                                  pS[:, 0:PAIRS].rearrange("p (s t h) -> p s t h", s=S, t=S),
                                  top[:, :].rearrange("p (s h) -> p s h", s=S).unsqueeze(2)
                                  .to_broadcast([P, S, S, H1]), ALU.subtract).then_inc(sem["shifted"], 1)

            def weigh(j, u, r):
                dve.wait_ge(sem["exps"], j + 1)
                dve.tensor_reduce(sums[:, :].rearrange("p (s h) -> p s h", s=S),
                                  exps[:, :].rearrange("p (s t h) -> p s h t", s=S, t=S), AX.X, ALU.add)\
                   .then_inc(sem["sums"], 1)
                dve.wait_ge(sem["sums"], j + 1)
                dve.reciprocal(inv[:, :], sums[:, :]).then_inc(sem["inv"], 1)
                dve.wait_ge(sem["inv"], j + 1)
                dve.tensor_tensor(att[:, :].rearrange("p (s t h) -> p s t h", s=S, t=S),
                                  exps[:, :].rearrange("p (s t h) -> p s t h", s=S, t=S),
                                  inv[:, :].rearrange("p (s h) -> p s h", s=S).unsqueeze(2)
                                  .to_broadcast([P, S, S, H1]), ALU.mult).then_inc(sem["att"], 1)
                dve.wait_ge(sem["att"], j + 1)
                dve.wait_ge(sem["v_sb"], j + 1)
                after(dve, sem["oT"], j)
                for s in range(S):
                    dve.tensor_tensor(
                        weighted[:, s * SB:(s + 1) * SB].rearrange("p (g d) -> p g d", d=HD1),
                        bcast_last(att[:, s * S * H1:(s + 1) * S * H1], HD1),
                        v[u][:, :].rearrange("p (g d) -> p g d", d=HD1), ALU.mult).then_inc(sem["weighted"], 1)

            def residual(j, u, r):
                dve.wait_ge(sem["proj"], j + 1)
                dve.wait_ge(sem["nb"], j + 1)
                after(dve, sem["zg"], j)
                dve.tensor_tensor(res[:, :], pW[:, :], nb[u][:, :], ALU.add).then_inc(sem["r"], 1)
                dve.wait_ge(sem["r"], j + 1)
                for s in range(S):
                    dve.bn_stats(stats1[:, s, :], res[:, s * D:(s + 1) * D]).then_inc(sem["stats1"], 1)
                dve.wait_ge(sem["stats1"], S * (j + 1))
                apart(dve)
                for s in range(S):
                    dve.bn_aggr(moments1[:, s, :], stats1[:, s, :]).then_inc(sem["moments1"], 1)

            def centre(j, u, r):
                dve.wait_ge(sem["std1"], j + 1)
                after(dve, sem["z"], S * j)
                dve.reciprocal(rstd1[:, :], std1[:, :]).then_inc(sem["rstd1"], 1)
                dve.wait_ge(sem["rstd1"], j + 1)
                for s in range(S):
                    dve.tensor_scalar(res[:, s * D:(s + 1) * D], res[:, s * D:(s + 1) * D], moments1[:, s, 0:1],
                                      rstd1[:, s:s + 1], ALU.subtract, ALU.mult).then_inc(sem["z"], 1)

            def keep_logits(j, u, r):
                dve.wait_ge(sem["logits"], j + 1)
                dve.tensor_copy(w["logits"][:, bass.ds(j * S * E, S * E)], pL).then_inc(sem["logits_sb"], 1)

            pipeline(dve, [(products, 1), (residual, 2), (statistics, 0), (shift, 1), (centre, 2), (normalise, 0),
                           (weigh, 1), (keep_logits, 2)],
                     NJ, 2, 4)

        @block.scalar
        def _(act):
            def exponent(j, u, r):
                act.wait_ge(sem["shifted"], j + 1)
                after(act, sem["att"], j)
                act.activation(exps[:, :], shifted[:, :], ACT.Exp, scale=HD1 ** -0.5).then_inc(sem["exps"], 1)

            def deviation(j, u, r):
                act.wait_ge(sem["moments"], S * (j + 1))
                after(act, sem["rstd"], j)
                act.activation(std[:, :], moments[u][:, :, 1], ACT.Sqrt, bias=w["eps"][:, :]).then_inc(sem["std"], 1)

            def deviation1(j, u, r):
                act.wait_ge(sem["moments1"], S * (j + 1))
                after(act, sem["rstd1"], j)
                act.activation(std1[:, :], moments1[:, :, 1], ACT.Sqrt, bias=w["eps"][:, :]).then_inc(sem["std1"], 1)

            def project(j, u, r):
                act.wait_ge(sem["nT"], j + 1)
                after(act, sem["v"], j - 1)
                act.activation(nT[u][:, :], pT[:, :], ACT.Copy).then_inc(sem["nT_sb"], 1)
                act.wait_ge(sem["q"], j + 1)
                after(act, sem["products"], S * (j - 1))
                act.activation(qT[u][:, :], pq[:, :], ACT.Identity, bias=w["bqkv"][:, 0:1]).then_inc(sem["q_sb"], 1)
                act.wait_ge(sem["k"], j + 1)
                act.activation(kT[u][:, :], pk[:, :], ACT.Identity, bias=w["bqkv"][:, 1:2]).then_inc(sem["k_sb"], 1)
                act.wait_ge(sem["v"], j + 1)
                after(act, sem["weighted"], S * (j - 1))
                act.activation(v[u][:, :], pv[:, :], ACT.Copy).then_inc(sem["v_sb"], 1)

            def outputs(j, u, r):
                act.wait_ge(sem["oT"], j + 1)
                after(act, sem["proj"], j)
                act.activation(oT[:, :], pO[:, :], ACT.Identity, bias=w["bqkv"][:, 2:3]).then_inc(sem["oT_sb"], 1)

            def turned_y(j, u, r):
                act.wait_ge(sem["yT"], j + 1)
                after(act, sem["logits"], j)
                act.activation(yT[:, :], pY[:, :], ACT.Copy).then_inc(sem["yT_sb"], 1)

            pipeline(act, [(deviation1, 2), (deviation, 0), (exponent, 1), (project, 0), (outputs, 1), (turned_y, 2)],
                     NJ, 2, 4)

        @block.tensor
        def _(pe):
            def scores(j, u, r):
                after(pe, sem["shifted"], j)
                after(pe, sem["logits_sb"], j - 2)
                for s in range(S):
                    pe.wait_ge(sem["products"], S * j + s + 1)
                    for t in range(S):
                        g = s * S + t
                        last = pe.matmul(pS[:, g * H1:(g + 1) * H1], prod[:, g * P:(g + 1) * P], c["heads"],
                                         start=True, stop=True)
                last.then_inc(sem["scores"], 1)

            def project(j, u, r):
                pe.wait_ge(sem["n"], S * (j + 1))
                after(pe, sem["nT_sb"], j)
                for s in range(S):
                    last = pe.transpose(pT[:, s * P:(s + 1) * P], n[u][:, s * D:(s + 1) * D], ident)
                last.then_inc(sem["nT"], 1)
                pe.wait_ge(sem["nT_sb"], j + 1)
                after(pe, sem["q_sb"], j)
                pe.matmul(pq[:, :], w["wqkv"][:, 0:D], nT[u][:, :], start=True, stop=True).then_inc(sem["q"], 1)
                after(pe, sem["k_sb"], j)
                pe.matmul(pk[:, :], w["wqkv"][:, D:2 * D], nT[u][:, :], start=True, stop=True).then_inc(sem["k"], 1)
                after(pe, sem["v_sb"], j)
                for s in range(S):
                    last = pe.matmul(pv[:, s * D:(s + 1) * D], nT[u][:, s * P:(s + 1) * P],
                                     w["wqkv"][:, 2 * D:3 * D], start=True, stop=True)
                last.then_inc(sem["v"], 1)

            def attended(j, u, r):
                after(pe, sem["oT_sb"], j)
                for s in range(S):
                    pe.wait_ge(sem["weighted"], S * j + s + 1)
                    for t in range(S):
                        g = s * S + t
                        last = pe.matmul(pO[:, s * P:(s + 1) * P], weighted[:, g * P:(g + 1) * P], ident,
                                         start=(t == 0), stop=(t == S - 1))
                last.then_inc(sem["oT"], 1)
                pe.wait_ge(sem["oT_sb"], j + 1)
                after(pe, sem["r"], j)
                for s in range(S):
                    last = pe.matmul(pW[:, s * D:(s + 1) * D], oT[:, s * P:(s + 1) * P], w["wo"][:, :],
                                     start=True, stop=True)
                last.then_inc(sem["proj"], 1)

            def router(j, u, r):
                pe.wait_ge(sem["y"], j + 1)
                after(pe, sem["yT_sb"], j)
                for s in range(S):
                    last = pe.transpose(pY[:, s * P:(s + 1) * P], yx[u][:, s, 0:D], ident)
                last.then_inc(sem["yT"], 1)
                pe.wait_ge(sem["yT_sb"], j + 1)
                if isinstance(j, int) and j + 1 >= NJ:
                    pe.wait_ge(sem["shifted"], NJ)
                else:
                    pe.wait_ge(sem["shifted"], j + 2)
                after(pe, sem["logits_sb"], j)
                for s in range(S):
                    last = pe.matmul(pL[:, s * E:(s + 1) * E], yT[:, s * P:(s + 1) * P], w["wg"][:, :],
                                     start=True, stop=True)
                last.then_inc(sem["logits"], 1)

            pipeline(pe, [(scores, 1), (project, 0), (attended, 1), (router, 2)], NJ, 2, 4)


def routing_phase(nc, c, w, tag):
    EG = E * NT
    with ExitStack() as ctx:
        def sb(name, shape, dt=F32):
            return ctx.enter_context(nc.sbuf_tensor(f"{tag}_{name}", shape, dt))

        sem = Names(nc, ctx, tag, "dve prefix inverse")
        best, tied, first = sb("best", [P, NT]), sb("tied", [P, EG]), sb("first", [P, NT])
        chosen, chosen16 = sb("chosen", [P, EG]), sb("chosen16", [P, EG], BF16)
        totals, summed, zeros = sb("totals", [P, EG]), sb("summed", [P, EG]), sb("zeros", [P, EG])
        count, full, tiles = sb("count", [P, E]), sb("full", [P, EG]), sb("tiles", [P, E])
        ends, shift = sb("ends", [P, E]), sb("shift", [P, E])
        slot, where = sb("slot_of", [P, EG]), sb("where", [P, NT])
        where_i, tile_i, lane_i = sb("where_i", [P, NT], I32), sb("tile_i", [P, NT], I32), sb("lane_i", [P, NT], I32)
        tile_f, lane_f = sb("tile_f", [P, NT]), sb("lane_f", [P, NT])
        passed, expert = sb("passed", [P, SLOTS * (E - 1)]), sb("expert_f", [P, SLOTS])
        lanes = sb("lanes", [P, NT * P], BF16)
        marks = sb("marks", [P, NT * 3 * SLOTS], BF16)
        inverse, reads, empty = sb("inverse", [P, 3 * SLOTS]), sb("reads_f", [P, SLOTS]), sb("empty", [P, SLOTS])
        writes = sb("writes_f", [P, SLOTS])
        pR = ctx.enter_context(nc.psum_tensor(f"{tag}_pPrefix", [P, 512], F32))
        pI = ctx.enter_context(nc.psum_tensor(f"{tag}_pInverse", [P, 512], F32))
        by_e = "p (e g) -> p e g"
        count_at = {}
        marks_v = marks[:, :].rearrange("p (g k t) -> p g k t", g=NT, k=3)
        block = ctx.enter_context(nc.Block())

        @block.vector
        def _(dve):
            done = [0]

            def then(instruction):
                done[0] += 1
                instruction.then_inc(sem["dve"], 1)
                dve.wait_ge(sem["dve"], done[0])

            logits = w["logits"][:, :].rearrange("p (g e) -> p g e", e=E)
            tied_v = tied[:, :].rearrange("p (g e) -> p g e", e=E)
            dve.memset(zeros[:, :], 0.0)
            then(dve.tensor_reduce(best[:, :], logits, AX.X, ALU.max))
            then(dve.tensor_tensor(tied_v, logits, bcast_last(best[:, :], E), ALU.is_ge))
            then(dve.tensor_tensor(tied_v, tied_v, bcast_mid(c["rank"], NT), ALU.mult))
            then(dve.tensor_reduce(first[:, :], tied_v, AX.X, ALU.max))
            then(dve.tensor_tensor(chosen[:, :].rearrange("p (e g) -> p g e", e=E),
                                   bcast_mid(c["rank"], NT), bcast_last(first[:, :], E), ALU.is_equal))
            then(dve.tensor_copy(chosen16[:, :], chosen[:, :]))
            count_at["chosen"] = done[0]
            dve.wait_ge(sem["prefix"], 1)
            then(dve.tensor_copy(totals[:, :], pR[:, EG:2 * EG]))
            then(dve.tensor_tensor_scan(summed[:, :], totals[:, :], zeros[:, :], 0.0, ALU.add, ALU.add))
            then(dve.tensor_reduce(count[:, :], totals[:, :].rearrange(by_e, e=E), AX.X, ALU.add))
            then(dve.tensor_tensor(full[:, :].rearrange(by_e, e=E), bcast_last(count[:, :], NT),
                                   bcast_mid(c["filled"], E), ALU.is_gt))
            then(dve.tensor_reduce(tiles[:, :], full[:, :].rearrange(by_e, e=E), AX.X, ALU.add))
            then(dve.tensor_tensor_scan(ends[:, :], tiles[:, :], zeros[:, 0:E], 0.0, ALU.add, ALU.add))
            then(dve.tensor_tensor(summed[:, :], summed[:, :], totals[:, :], ALU.subtract))
            then(dve.tensor_tensor(shift[:, :], ends[:, :], tiles[:, :], ALU.subtract))
            then(dve.scalar_tensor_tensor(shift[:, :], shift[:, :], float(P),
                                          summed[:, :].rearrange(by_e, e=E)[:, :, 0], ALU.mult, ALU.subtract))
            then(dve.tensor_tensor(slot[:, :], summed[:, :], pR[:, 0:EG], ALU.add))
            then(dve.tensor_tensor(slot[:, :].rearrange(by_e, e=E), slot[:, :].rearrange(by_e, e=E),
                                   bcast_last(shift[:, :], NT), ALU.add))
            then(dve.tensor_tensor(slot[:, :], slot[:, :], chosen[:, :], ALU.mult))
            then(dve.tensor_reduce(where[:, :], slot[:, :].rearrange("p (e g) -> p g e", e=E), AX.X, ALU.add))
            then(dve.tensor_copy(where_i[:, :], where[:, :]))
            then(dve.tensor_scalar(tile_i[:, :], where_i[:, :], 7, None, ALU.logical_shift_right))
            then(dve.tensor_scalar(lane_i[:, :], where_i[:, :], P - 1, None, ALU.bitwise_and))
            then(dve.tensor_copy(tile_f[:, :], tile_i[:, :]))
            then(dve.tensor_copy(lane_f[:, :], lane_i[:, :]))
            then(dve.tensor_tensor(passed[:, :].rearrange("p (t e) -> p t e", e=E - 1), bcast_last(c["slot"], E - 1),
                                   bcast_mid(ends[:, 0:E - 1], SLOTS), ALU.is_ge))
            then(dve.tensor_reduce(expert[:, :], passed[:, :].rearrange("p (t e) -> p t e", e=E - 1), AX.X, ALU.add))
            then(dve.tensor_copy(w["expert"][:, :], expert[:, :]))
            then(dve.tensor_tensor(lanes[:, :].rearrange("p (g l) -> p g l", g=NT), bcast_mid(c["lane"], NT),
                                   bcast_last(lane_f[:, :], P), ALU.is_equal))
            then(dve.tensor_tensor(marks_v[:, :, 2, :], bcast_mid(c["slot"], NT), bcast_last(tile_f[:, :], SLOTS),
                                   ALU.is_equal))
            then(dve.tensor_scalar(marks_v[:, :, 0, :], marks_v[:, :, 2, :], c["part"], None, ALU.mult))
            then(dve.tensor_tensor(marks_v[:, :, 1, :], marks_v[:, :, 2, :], bcast_last(c["high"], SLOTS), ALU.mult))
            count_at["marks"] = done[0]
            dve.wait_ge(sem["inverse"], 1)
            then(dve.tensor_copy(inverse[:, :], pI[:, 0:3 * SLOTS]))
            low, high, used = [inverse[:, k * SLOTS:(k + 1) * SLOTS] for k in range(3)]
            then(dve.scalar_tensor_tensor(reads[:, :], high, float(P), low, ALU.mult, ALU.add))
            then(dve.tensor_scalar(empty[:, :], used, -1.0, 1.0, ALU.mult, ALU.add))
            then(dve.tensor_tensor(empty[:, :], empty[:, :], c["spare"], ALU.mult))
            then(dve.tensor_tensor(writes[:, :], reads[:, :], empty[:, :], ALU.add))
            then(dve.tensor_copy(w["reads"][:, :], reads[:, :]))
            then(dve.tensor_copy(w["writes"][:, :], writes[:, :]))

        @block.tensor
        def _(pe):
            pe.wait_ge(sem["dve"], count_at["chosen"])
            pe.matmul(pR[:, 0:EG], w["before16"][:, :], chosen16[:, :], start=True, stop=True)
            pe.matmul(pR[:, EG:2 * EG], w["ones16"][:, :], chosen16[:, :], start=True, stop=True)\
              .then_inc(sem["prefix"], 1)
            pe.wait_ge(sem["dve"], count_at["marks"])

            def locate(g, start, stop):
                return pe.matmul(pI[:, 0:3 * SLOTS], lanes[:, bass.ds(g * P, P)],
                                 marks[:, bass.ds(g * 3 * SLOTS, 3 * SLOTS)], start=start, stop=stop)

            locate(0, True, False)
            with pe.Fori(1, NT - 1, 1) as g:
                locate(g, False, False)
            locate(NT - 1, False, True).then_inc(sem["inverse"], 1)


def experts_phase(nc, c, w, dram, dst, tag):
    with ExitStack() as ctx:
        def sb(name, shape, dt=F32):
            return ctx.enter_context(nc.sbuf_tensor(f"{tag}_{name}", shape, dt))

        def some(k, name, shape, dt=F32):
            return [sb(f"{name}_{b}", shape, dt) for b in range(k)]

        def bank(name):
            return ctx.enter_context(nc.psum_tensor(f"{tag}_{name}", [P, 512], F32))

        sem = Names(nc, ctx, tag, "index gathered*8 w1 yT yT_sb h hb hT o a stats moments std rstd zg out "
                    "out_index scattered*8")
        index, out_index = some(8, "index", [P, 1], I32), some(8, "out_index", [P, 1], I32)
        rows = some(8, "rows", [P, 2 * D])
        out = some(8, "out", [P, D])
        w1 = some(2, "w1", [P, DF])
        yT, hb, hT = some(4, "yT", [P, P]), some(2, "hb", [P, DF]), some(2, "hT", [P, DF])
        a, zg = sb("a", [P, D]), sb("zg", [P, D])
        stats, moments, rstd, std = sb("stats", [P, 6]), sb("moments", [P, 2]), sb("rstd", [P, 1]), sb("std", [P, 1])
        pT, pH, pO = bank("turn"), [bank("h0"), bank("h1")], [bank("o0"), bank("o1")]
        ident = c["ident"]
        block = ctx.enter_context(nc.Block())

        @block.gpsimd
        def _(pool):
            def gather(t, u, r):
                pool.wait_ge(sem["index"], t + 1)
                after(pool, sem["out"], t - 7)
                apart(pool)
                pool.indirect_dma_start(rows[u][:, :], None, dram["yx"],
                                        bass.IndirectOffsetOnAxis(ap=index[u][:, :], axis=0))\
                    .then_inc(sem[f"gathered{u}"], 16)

            def scatter(t, u, r):
                pool.wait_ge(sem["out_index"], t + 1)
                pool.wait_ge(sem["out"], t + 1)
                apart(pool)
                pool.indirect_dma_start(dst, bass.IndirectOffsetOnAxis(ap=out_index[u][:, :], axis=0),
                                        out[u][:, :], None).then_inc(sem[f"scattered{u}"], 16)

            pipeline(pool, [(gather, 0), (scatter, 6)], SLOTS, 8, 8)
            for u in range(8):
                pool.wait_ge(sem[f"scattered{u}"], 16 * (SLOTS // 8))

        @block.scalar
        def _(act):
            experts = Experts(nc, w, mybir.EngineType.Activation, [2])

            def weights(t, u, r):
                e = experts.of(2)
                after(act, sem["h"], t - 1)
                act.activation(w1[u % 2][:, :], w["w1"][:, bass.ds(e * DF, DF)], ACT.Copy).then_inc(sem["w1"], 1)

            def turned(t, u, r):
                act.wait_ge(sem["yT"], t + 1)
                after(act, sem["o"], t - 3)
                act.activation(yT[u % 4][:, :], pT[:, 0:P], ACT.Copy).then_inc(sem["yT_sb"], 1)

            def relu(t, u, r):
                act.wait_ge(sem["hb"], t + 1)
                after(act, sem["o"], t - 1)
                act.activation(hT[u % 2][:, :], hb[u % 2][:, :], ACT.Relu).then_inc(sem["hT"], 1)

            def deviation(t, u, r):
                act.wait_ge(sem["moments"], t + 1)
                after(act, sem["rstd"], t)
                act.activation(std[:, :], moments[:, 1:2], ACT.Sqrt, bias=w["eps"][:, :]).then_inc(sem["std"], 1)

            pipeline(act, [(relu, 4), (weights, 2), (deviation, 5), (turned, 2)], SLOTS, 8, 8, experts)

        @block.tensor
        def _(pe):
            experts = Experts(nc, w, mybir.EngineType.PE, [4])

            def turn(t, u, r):
                pe.wait_ge(sem[f"gathered{u}"], 16 * (r + 1))
                after(pe, sem["yT_sb"], t)
                pe.transpose(pT[:, 0:P], rows[u][:, 0:D], ident).then_inc(sem["yT"], 1)

            def up(t, u, r):
                pe.wait_ge(sem["w1"], t + 1)
                pe.wait_ge(sem["yT_sb"], t + 1)
                after(pe, sem["hb"], t - 1)
                for k in range(NC):
                    last = pe.matmul(pH[u % 2][:, k * P:(k + 1) * P], w1[u % 2][:, k * P:(k + 1) * P],
                                     yT[u % 4][:, :], start=True, stop=True)
                last.then_inc(sem["h"], 1)

            def down(t, u, r):
                e = experts.of(4)
                pe.wait_ge(sem["hT"], t + 1)
                after(pe, sem["a"], t - 1)
                for k in range(NC):
                    last = pe.matmul(pO[u % 2][:, 0:D], hT[u % 2][:, k * P:(k + 1) * P],
                                     w["w2"][:, bass.ds(e * DF + k * D, D)], start=(k == 0), stop=False)
                last = pe.matmul(pO[u % 2][:, 0:D], yT[u % 4][:, :], ident, start=False, stop=True)
                last.then_inc(sem["o"], 1)

            pipeline(pe, [(up, 3), (turn, 2), (down, 4)], SLOTS, 8, 8, experts)

        @block.vector
        def _(dve):
            experts = Experts(nc, w, mybir.EngineType.DVE, [3, 5])

            def bias(t, u, r):
                e = experts.of(3)
                dve.wait_ge(sem["h"], t + 1)
                after(dve, sem["hT"], t - 1)
                dve.tensor_tensor(hb[u % 2][:, :].rearrange("p (k b) -> p k b", k=NC),
                                  pH[u % 2][:, :].rearrange("p (k b) -> p k b", k=NC),
                                  bcast_last(w["b1"][:, bass.ds(e * NC, NC)], P), ALU.add).then_inc(sem["hb"], 1)

            def indices(t, u, r):
                after(dve, sem[f"gathered{u}"], 16 * r)
                dve.tensor_copy(index[u][:, :], w["reads"][:, bass.ds(t, 1)]).then_inc(sem["index"], 1)

            def out_indices(t, u, r):
                after(dve, sem[f"scattered{u}"], 16 * r)
                dve.tensor_copy(out_index[u][:, :], w["writes"][:, bass.ds(t, 1)]).then_inc(sem["out_index"], 1)

            def statistics(t, u, r):
                e = experts.of(5)
                dve.wait_ge(sem["o"], t + 1)
                dve.tensor_tensor(a[:, :], pO[u % 2][:, 0:D], w["b2"][:, bass.ds(e * D, D)], ALU.add)\
                   .then_inc(sem["a"], 1)
                dve.wait_ge(sem["a"], t + 1)
                dve.bn_stats(stats[:, :], a[:, :]).then_inc(sem["stats"], 1)
                dve.wait_ge(sem["stats"], t + 1)
                apart(dve)
                dve.bn_aggr(moments[:, :], stats[:, :]).then_inc(sem["moments"], 1)
                dve.wait_ge(sem["moments"], t + 1)
                dve.scalar_tensor_tensor(zg[:, :], a[:, :], moments[:, 0:1], w["g2h"][:, :],
                                         ALU.subtract, ALU.mult).then_inc(sem["zg"], 1)

            def finish(t, u, r):
                dve.wait_ge(sem["std"], t + 1)
                dve.reciprocal(rstd[:, :], std[:, :]).then_inc(sem["rstd"], 1)
                dve.wait_ge(sem["rstd"], t + 1)
                dve.wait_ge(sem["zg"], t + 1)
                after(dve, sem[f"scattered{u}"], 16 * r)
                dve.scalar_tensor_tensor(out[u][:, :], zg[:, :], rstd[:, 0:1], rows[u][:, D:2 * D],
                                         ALU.mult, ALU.add).then_inc(sem["out"], 1)

            pipeline(dve, [(indices, 0), (statistics, 5), (bias, 3), (out_indices, 5), (finish, 5)], SLOTS, 8, 8, experts)


def linear_attention_phase(nc, c, w, src, tag):
    QK = 2 * D
    KV = H2 * HM * HD2
    PIECES = [(0, 6), (6, 11), (11, 16)]
    LOADED = 4
    with ExitStack() as ctx:
        def sb(name, shape, dt=F32):
            return ctx.enter_context(nc.sbuf_tensor(f"{tag}_{name}", shape, dt))

        def some(k, name, shape, dt=F32):
            return [sb(f"{name}_{b}", shape, dt) for b in range(k)]

        def bank(name):
            return ctx.enter_context(nc.psum_tensor(f"{tag}_bank_{name}", [P, 512], F32))

        sem = Names(nc, ctx, tag, "x_loaded stats moments std rstd n nT nT_sb qkv qk_sb v_sb rc rs rot relu "
                    "kv cum prod num den inv o oT oT_sb proj out")
        x = w["x"]
        n = some(2, "n", [P, D])
        stats, moments, rstd, std = sb("stats", [P, 6]), sb("moments", [P, 2]), sb("rstd", [P, 1]), sb("std", [P, 1])
        nT = sb("nT", [P, P])
        qk, rc, rs, rot = some(2, "qk", [P, QK]), sb("rc", [P, QK]), sb("rs", [P, QK]), sb("rot", [P, QK])
        relu = some(4, "relu", [P, QK])
        values = w["values"]
        kv, prod = some(4, "kv", [P, KV]), sb("prod", [P, KV])
        num, den, inv = sb("num", [P, H2 * HM]), sb("den", [P, H2]), sb("inv", [P, H2])
        o, oT = some(4, "o", [P, D]), sb("oT", [P, P])
        pN, pQ, pT, pO, pA, pB, pC = [bank(name) for name in ["nT", "qkv", "oT", "proj", "sumA", "sumB", "sumC"]]
        pieces = [pA, pB, pC]
        ident = c["ident"]
        hm = "p (h m) -> p h m"
        block = ctx.enter_context(nc.Block())

        @block.sync
        def _(sp):
            for g in range(NT // LOADED):
                sp.dma_start(x[:, g * LOADED * D:(g + 1) * LOADED * D].rearrange("p (t d) -> p t d", d=D),
                             src[g * LOADED * P:(g + 1) * LOADED * P, :].rearrange("(t p) d -> p t d", p=P))\
                  .then_inc(sem["x_loaded"], 16)
                sp.wait_ge(sem["x_loaded"], 16 * (g + 1))

        @block.vector
        def _(dve):
            def statistics(t, u, r):
                if isinstance(t, int):
                    loaded = 16 * (t // LOADED + 1)
                else:
                    loaded = 16 * (r * (NJ // LOADED) + u // LOADED + 1)
                dve.wait_ge(sem["x_loaded"], loaded)
                apart(dve)
                after(dve, sem["moments"], t)
                dve.bn_stats(stats[:, :], x[:, bass.ds(t * D, D)]).then_inc(sem["stats"], 1)

            def aggregate(t, u, r):
                dve.wait_ge(sem["stats"], t + 1)
                after(dve, sem["n"], t)
                apart(dve)
                dve.bn_aggr(moments[:, :], stats[:, :]).then_inc(sem["moments"], 1)

            def inverse(t, u, r):
                dve.wait_ge(sem["std"], t + 1)
                after(dve, sem["n"], t)
                dve.reciprocal(rstd[:, :], std[:, :]).then_inc(sem["rstd"], 1)

            def normalise(t, u, r):
                dve.wait_ge(sem["rstd"], t + 1)
                after(dve, sem["nT"], t - 1)
                dve.tensor_scalar(n[u % 2][:, :], x[:, bass.ds(t * D, D)], moments[:, 0:1], rstd[:, 0:1],
                                  ALU.subtract, ALU.mult).then_inc(sem["n"], 1)

            def multiply(k):
                def piece(t, u, r):
                    h0, h1 = PIECES[k]
                    dve.wait_ge(sem["cum"], 3 * t + k + 1)
                    after(dve, sem["num"], t)
                    q = relu[u % 4][:, h0 * HD2:h1 * HD2].rearrange("p (h d) -> p h d", d=HD2)
                    size = [P, h1 - h0, HM, HD2]
                    dve.tensor_tensor(
                        prod[:, h0 * HM * HD2:h1 * HM * HD2].rearrange("p (h m d) -> p h m d", m=HM, d=HD2),
                        pieces[k][:, 0:(h1 - h0) * HM * HD2].rearrange("p (h m d) -> p h m d", m=HM, d=HD2),
                        q.unsqueeze(2).to_broadcast(size), ALU.mult).then_inc(sem["prod"], 1)
                return piece

            def total(t, u, r):
                dve.wait_ge(sem["prod"], 3 * (t + 1))
                after(dve, sem["o"], t)
                dve.tensor_reduce(num[:, :], prod[:, :].rearrange("p (g d) -> p g d", d=HD2), AX.X, ALU.add)\
                   .then_inc(sem["num"], 1)

            def divide(t, u, r):
                dve.wait_ge(sem["num"], t + 1)
                num_v = num[:, :].rearrange(hm, m=HM)
                dve.tensor_scalar(den[:, :], num_v[:, :, HD2], EPS_LA, None, ALU.add).then_inc(sem["den"], 1)
                dve.wait_ge(sem["den"], t + 1)
                dve.reciprocal(inv[:, :], den[:, :]).then_inc(sem["inv"], 1)
                dve.wait_ge(sem["inv"], t + 1)
                after(dve, sem["oT"], t - 3)
                dve.tensor_tensor(o[u % 4][:, :].rearrange("p (h m) -> p h m", m=HD2), num_v[:, :, 0:HD2],
                                  bcast_last(inv[:, :], HD2), ALU.mult).then_inc(sem["o"], 1)

            def finish(t, u, r):
                dve.wait_ge(sem["proj"], t + 1)
                apart(dve)
                here = x[:, bass.ds(t * D, D)]
                dve.tensor_tensor(here, pO[:, 0:D], here, ALU.add).then_inc(sem["out"], 1)

            pipeline(dve, [(finish, 7), (statistics, 0), (multiply(0), 4), (aggregate, 0), (multiply(1), 4),
                           (inverse, 0), (multiply(2), 4), (normalise, 0), (total, 4), (divide, 4)], NT, 8, 8)

        @block.gpsimd
        def _(pool):
            def rotate(t, u, r):
                pool.wait_ge(sem["qk_sb"], t + 1)
                after(pool, sem["rot"], t)
                heads = [P, 2 * H2, HD2]
                cos = bcast_mid(c["cos"][:, u * HD2:(u + 1) * HD2], 2 * H2)
                sin = c["sin"][:, u * HD2:(u + 1) * HD2].rearrange("p (i two) -> p i two", two=2)
                pairs = "p (h i two) -> p h i two"
                pool.tensor_tensor(rc[:, :].rearrange("p (h d) -> p h d", d=HD2),
                                   qk[u % 2][:, :].rearrange("p (h d) -> p h d", d=HD2), cos, ALU.mult)\
                    .then_inc(sem["rc"], 1)
                for side in range(2):
                    pool.tensor_tensor(rs[:, :].rearrange(pairs, i=HD2 // 2, two=2)[:, :, :, side],
                                       qk[u % 2][:, :].rearrange(pairs, i=HD2 // 2, two=2)[:, :, :, 1 - side],
                                       bcast_mid(sin[:, :, side], 2 * H2), ALU.mult).then_inc(sem["rs"], 1)
                pool.wait_ge(sem["rc"], t + 1)
                pool.wait_ge(sem["rs"], 2 * (t + 1))
                after(pool, sem["relu"], t)
                pool.tensor_tensor(rot[:, :], rc[:, :], rs[:, :], ALU.add).then_inc(sem["rot"], 1)

            def outer(t, u, r):
                pool.wait_ge(sem["relu"], t + 1)
                pool.wait_ge(sem["v_sb"], t + 1)
                after(pool, sem["cum"], 3 * (t - 2))
                size = [P, H2, HM, HD2]
                k = relu[u % 4][:, D:QK].rearrange("p (h d) -> p h d", d=HD2)
                pool.tensor_tensor(kv[u % 4][:, :].rearrange("p (h m d) -> p h m d", m=HM, d=HD2),
                                   k.unsqueeze(2).to_broadcast(size),
                                   bcast_last(values[u % 4][:, :].rearrange(hm, m=HM), HD2), ALU.mult)\
                    .then_inc(sem["kv"], 1)

            pipeline(pool, [(rotate, 2), (outer, 3)], NT, 8, 8)

        @block.scalar
        def _(act):
            def turned(t, u, r):
                act.wait_ge(sem["nT"], t + 1)
                after(act, sem["qkv"], t)
                act.activation(nT[:, :], pN[:, 0:P], ACT.Copy).then_inc(sem["nT_sb"], 1)

            def project(t, u, r):
                act.wait_ge(sem["qkv"], t + 1)
                after(act, sem["rc"], t - 1)
                after(act, sem["rs"], 2 * (t - 1))
                act.activation(qk[u % 2][:, :], pQ[:, 0:QK], ACT.Copy).then_inc(sem["qk_sb"], 1)
                after(act, sem["kv"], t - 3)
                act.activation(values[u % 4][:, :].rearrange(hm, m=HM)[:, :, 0:HD2],
                               pQ[:, QK:QK + D].rearrange("p (h m) -> p h m", m=HD2), ACT.Copy)\
                   .then_inc(sem["v_sb"], 1)

            def rectify(t, u, r):
                act.wait_ge(sem["rot"], t + 1)
                after(act, sem["kv"], t - 3)
                after(act, sem["prod"], 3 * (t - 3))
                act.activation(relu[u % 4][:, :], rot[:, :], ACT.Relu).then_inc(sem["relu"], 1)

            def outputs(t, u, r):
                act.wait_ge(sem["oT"], t + 1)
                after(act, sem["proj"], t)
                act.activation(oT[:, :], pT[:, 0:P], ACT.Copy).then_inc(sem["oT_sb"], 1)

            def deviation(t, u, r):
                act.wait_ge(sem["moments"], t + 1)
                after(act, sem["rstd"], t)
                act.activation(std[:, :], moments[:, 1:2], ACT.Sqrt, bias=w["eps"][:, :]).then_inc(sem["std"], 1)

            pipeline(act, [(turned, 1), (deviation, 0), (rectify, 2), (project, 1), (outputs, 6)], NT, 8, 8)

        @block.tensor
        def _(pe):
            def turn(t, u, r):
                pe.wait_ge(sem["n"], t + 1)
                after(pe, sem["nT_sb"], t)
                pe.transpose(pN[:, 0:P], n[u % 2][:, :], ident).then_inc(sem["nT"], 1)

            def running(k):
                def piece(t, u, r):
                    h0, h1 = PIECES[k]
                    columns = slice(h0 * HM * HD2, h1 * HM * HD2)
                    size = (h1 - h0) * HM * HD2
                    after(pe, sem["prod"], 3 * (t - 1) + k + 1)
                    if u > 0:
                        pe.matmul(pieces[k][:, 0:size], c["later"], kv[(u - 1) % 4][:, columns],
                                  start=False, stop=False, skip_group_check=True)
                    pe.wait_ge(sem["kv"], t + 1)
                    pe.matmul(pieces[k][:, 0:size], c["upto"], kv[u % 4][:, columns],
                              start=(u == 0), stop=True, skip_group_check=True).then_inc(sem["cum"], 1)
                return piece

            def project(t, u, r):
                pe.wait_ge(sem["nT_sb"], t + 1)
                after(pe, sem["v_sb"], t)
                pe.matmul(pQ[:, 0:3 * D], nT[:, :], w["la_wqkv"][:, :], start=True, stop=True)\
                  .then_inc(sem["qkv"], 1)

            def output(t, u, r):
                pe.wait_ge(sem["o"], t + 1)
                after(pe, sem["oT_sb"], t)
                pe.transpose(pT[:, 0:P], o[u % 4][:, :], ident).then_inc(sem["oT"], 1)

            def combine(t, u, r):
                pe.wait_ge(sem["oT_sb"], t + 1)
                after(pe, sem["out"], t)
                pe.matmul(pO[:, 0:D], oT[:, :], w["la_wo"][:, :], start=True, stop=True)\
                  .then_inc(sem["proj"], 1)

            pipeline(pe, [(running(0), 4), (turn, 1), (output, 6), (running(1), 4), (project, 1), (running(2), 4),
                          (combine, 6)], NT, 8, 8)


def copy_out(nc, dram, out):
    with ExitStack() as ctx:
        copied = ctx.enter_context(nc.semaphore("copied"))
        block = ctx.enter_context(nc.Block())

        @block.sync
        def _(sp):
            sp.dma_start(out.rearrange("s l d -> (s l) d"), dram["x3"][0:N, :]).then_inc(copied, 16)
            sp.wait_ge(copied, 16)


def macaron_kernel(nc, dram, out):
    where, width = const_columns()
    with ExitStack() as ctx:
        def sb(name, shape, dt=F32):
            return ctx.enter_context(nc.sbuf_tensor(f"w_{name}", shape, dt))

        w = {name: sb(name, shape) for name, shape in [
            ("const", [P, width]), ("wqkv", [P, 3 * D]), ("wo", [P, D]), ("wg", [P, E]), ("bqkv", [P, 3]),
            ("w1", [P, E * DF]), ("w2", [P, E * DF]), ("b1", [P, E * NC]), ("b2", [P, E * D]),
            ("la_wqkv", [P, 3 * D]), ("la_wo", [P, D]), ("bo", [P, D]), ("g1", [P, D]), ("be1", [P, D]),
            ("g2", [P, D]), ("be2", [P, D]), ("g2h", [P, D]), ("be2h", [P, D]), 
            ("eps", [P, 1]), ("x", [P, NT * D]), ("logits", [P, NT * E])]}
        w["before16"], w["ones16"] = sb("before16", [P, P], BF16), sb("ones16", [P, P], BF16)
        for name in ["expert", "reads", "writes"]:
            w[name] = sb(name, [P, SLOTS], I32)
        w["values"] = [sb(f"values{b}", [P, H2 * HM]) for b in range(4)]
        c = {name: w["const"][:, a:b] for name, (a, b) in where.items()}
        dram["yx"] = nc.dram_tensor("rows_yx", [N, 2 * D], F32, kind="Internal").ap()
        dram["x1"] = nc.dram_tensor("rows_x1", [N + SPARE, D], F32, kind="Internal").ap()
        dram["x3"] = nc.dram_tensor("rows_x3", [N + SPARE, D], F32, kind="Internal").ap()
        load_constants(nc, c, w, dram)
        attention_phase(nc, c, w, dram, "a1", True)
        routing_phase(nc, c, w, "r1")
        experts_phase(nc, c, w, dram, dram["x1"], "e1")
        linear_attention_phase(nc, c, w, dram["x1"], "la")
        attention_phase(nc, c, w, dram, "a2", False)
        routing_phase(nc, c, w, "r2")
        experts_phase(nc, c, w, dram, dram["x3"], "e2")
        copy_out(nc, dram, out)


def shape_constants():
    import numpy as np
    where, width = const_columns()
    table = np.zeros((P, width), np.float32)

    def put(name, a):
        table[:, where[name][0]:where[name][1]] = a

    i = np.arange(P)
    put("ident", np.eye(P))
    put("upto", i[:, None] <= i[None, :])
    put("before", i[:, None] < i[None, :])
    put("later", i[:, None] > i[None, :])
    put("ones", 1.0)
    put("heads", i[:, None] // HD1 == np.arange(H1)[None, :])
    put("lane", i[None, :])
    put("slot", np.arange(SLOTS)[None, :])
    put("filled", (P * np.arange(NT))[None, :])
    put("rank", (E - np.arange(E))[None, :])
    put("part", i[:, None])
    put("spare", N + i[:, None] + P * np.arange(SLOTS)[None, :])
    g = np.arange(NT)
    put("high", ((g % S) * NJ + g // S)[None, :])
    inv_freq = (np.float32(1.0) / np.power(np.float32(10000.0), np.arange(0, HD2, 2, dtype=np.float32) / np.float32(HD2))).astype(np.float32)
    freqs = np.arange(L, dtype=np.float32)[:, None] * inv_freq[None, :]
    cos = np.cos(freqs.astype(np.float64)).astype(np.float32)
    sin = np.sin(freqs.astype(np.float64)).astype(np.float32)
    cos2 = np.repeat(cos, 2, axis=1)
    sin2 = np.stack([-sin, sin], axis=2).reshape(L, HD2)
    put("cos", cos2.reshape(NJ, P, HD2).transpose(1, 0, 2).reshape(P, NJ * HD2))
    put("sin", sin2.reshape(NJ, P, HD2).transpose(1, 0, 2).reshape(P, NJ * HD2))
    return table


def kernel(**inputs):
    import numpy as np
    import concourse.bacc as bacc
    from concourse.bass_utils import run_bass_kernel_spmd

    def lay(name):
        return np.asarray(inputs[name])

    arrays = {
        "x": lay("L0_attn_x").reshape(N, D),
        "wqkv": lay("L0_ffn_Wqkv").T, "wo": lay("L0_ffn_Wo").T, "wg": lay("L0_ffn_Wg").T,
        "bqkv": lay("L0_ffn_bqkv").reshape(3, D).T, "w1": lay("L0_ffn_W1"), "w2": lay("L0_ffn_W2"),
        "b1": lay("L0_ffn_b1").reshape(E * NC, P).T, "b2": lay("L0_ffn_b2"), "bo": lay("L0_ffn_bo"),
        "g1": lay("L0_ffn_g1"), "be1": lay("L0_ffn_be1"), "g2": lay("L0_ffn_g2"), "be2": lay("L0_ffn_be2"),
        "la_wq": lay("L0_attn_wq"), "la_wk": lay("L0_attn_wk"), "la_wv": lay("L0_attn_wv"),
        "la_wo": lay("L0_attn_wo"), "const": shape_constants(),
    }
    nc = bacc.Bacc("TRN2", target_bir_lowering=False, num_devices=1)
    sent, dram = {}, {}
    for name, a in arrays.items():
        sent[f"in_{name}"] = np.ascontiguousarray(a)
        dram[name] = nc.dram_tensor(f"in_{name}", list(a.shape), F32, kind="ExternalInput").ap()
    out = nc.dram_tensor("out", [S, L, D], F32, kind="ExternalOutput").ap()
    macaron_kernel(nc, dram, out)
    r = run_bass_kernel_spmd(nc, [sent], core_ids=[0])
    return r.results[0]["out"]
```

```python
import concourse.bass as bass
from concourse import mybir
from contextlib import ExitStack

F32 = mybir.dt.float32
BF16 = mybir.dt.bfloat16
I32 = mybir.dt.int32
ALU = mybir.AluOpType
ACT = mybir.ActivationFunctionType
AX = mybir.AxisListType

P = 128
D = 128
S = 4
L = 1024
N = S * L
NJ = L // P
NT = N // P
H1, HD1 = 4, 32
H2, HD2 = 16, 8
HM = HD2 + 1
E, DF = 8, 512
NC = DF // P
SLOTS = NT + E
SPARE = SLOTS * P
EPS_LN, EPS_LA = 1e-5, 1e-6
PAIRS = S * S * H1

CONST_PARTS = [("ident", P), ("upto", P), ("before", P), ("later", P), ("ones", P), ("heads", H1),
               ("lane", P), ("slot", SLOTS), ("filled", NT), ("rank", E), ("part", 1), ("spare", SLOTS),
               ("high", NT), ("cos", NJ * HD2), ("sin", NJ * HD2)]


EARLY_PARTS = [("wqkv", 3 * D), ("wo", D), ("wg", E), ("bqkv", 3)]
LATE_PARTS = [("la_wqkv", 3 * D), ("la_wo", D), ("b1", E * NC)]
ROWS = ["bo", "g1", "be1", "g2", "be2"]
EARLY_WIDTH, LATE_WIDTH = sum(n for _, n in EARLY_PARTS), sum(n for _, n in LATE_PARTS)


def const_columns():
    at, where = 0, {}
    for name, width in CONST_PARTS:
        where[name] = (at, at + width)
        at += width
    return where, at


def after(engine, semaphore, count):
    if isinstance(count, int) and count <= 0:
        return
    engine.wait_ge(semaphore, count)


def apart(engine):
    engine.nop(nofuse=True)


def pipeline(engine, stages, count, unroll, first, experts=None):
    depth = max(lag for _, lag in stages)
    loops = (count - first) // unroll

    def load(i, n):
        if experts:
            experts.load(i, n)

    def peeled(i):
        if experts:
            experts.step += 1
        for stage, lag in stages:
            if 0 <= i - lag < count:
                stage(i - lag, (i - lag) % unroll, (i - lag) // unroll)

    load(0, first)
    for i in range(first):
        peeled(i)
    with engine.Fori(0, loops, 1) as turn:
        load(turn * unroll + first, unroll)
        for k in range(unroll):
            if experts:
                experts.step += 1
            for stage, lag in stages:
                at = first + k - lag
                stage(turn * unroll + at, at % unroll, turn + at // unroll)
    load(first + loops * unroll, count + depth - first - loops * unroll)
    for i in range(first + loops * unroll, count + depth):
        peeled(i)


def straight(stages, count, buffers):
    for i in range(count + max(lag for _, lag in stages)):
        for stage, lag in stages:
            if 0 <= i - lag < count:
                stage(i - lag, (i - lag) % buffers, (i - lag) // buffers)


def bcast_mid(ap, n):
    return ap.unsqueeze(1).to_broadcast([ap.shape[0], n, ap.shape[1]])


def bcast_last(ap, n):
    return ap.unsqueeze(len(ap.shape)).to_broadcast(list(ap.shape) + [n])


class Experts:

    def __init__(self, nc, w, engine, lags):
        self.nc, self.w, self.engine, self.lags = nc, w, engine, lags

    def load(self, i, n):
        lo, hi = i - max(self.lags), i + n - min(self.lags)
        if isinstance(i, int):
            lo, hi = max(lo, 0), min(hi, SLOTS)
            count = hi - lo
        else:
            count = n + max(self.lags) - min(self.lags)
        _, self.values = self.nc.values_load_multi_w_load_instructions(
            self.w["expert"][0:1, bass.ds(lo, count)], engines=[self.engine], min_val=0, max_val=E - 1,
            skip_runtime_bounds_check_because="an expert is a sum of E - 1 values that are 0 or 1")
        self.skipped = lo - (i - max(self.lags)) if isinstance(i, int) else 0
        self.step = -1

    def of(self, lag):
        return self.values[self.step + max(self.lags) - lag - self.skipped]


class Names:

    def __init__(self, nc, ctx, phase, names):
        self.of = {}
        ctx.callback(self.clear, nc)
        for entry in names.split():
            name, _, k = entry.partition("*")
            for n in [f"{name}{b}" for b in range(int(k))] if k else [name]:
                self.of[n] = nc.alloc_semaphore(f"{phase}_{n}")

    def clear(self, nc):
        nc.clear_and_free_semaphores(list(self.of.values()))
        nc.all_engine_barrier()

    def __getitem__(self, name):
        return self.of[name]


def load_phase(nc, c, w, dram):
    with ExitStack() as ctx:
        sem = Names(nc, ctx, "load", "x_loaded*4 loaded be2h stats moments")
        EARLY = 3
        stats = ctx.enter_context(nc.sbuf_tensor("load_stats", [P, NT * 6], F32))
        x_all = w["x"][:, :].rearrange("p (s j d) -> p s j d", s=S, d=D)
        x_dram = dram["x"].rearrange("(s l) d -> l s d", s=S)
        block = ctx.enter_context(nc.Block())

        @block.sync
        def _(sp):
            for j in range(NJ):
                if j >= 4:
                    sp.wait_ge(sem[f"x_loaded{j % 4}"], 16 * (j // 4))
                sp.dma_start(x_all[:, :, j, :], x_dram[j * P:(j + 1) * P, :, :]).then_inc(sem[f"x_loaded{j % 4}"], 16)

        @block.scalar
        def _(act):
            act.dma_start(w["early"][:, :], dram["early"]).then_inc(sem["loaded"], 16)
            act.dma_start(w["rows"][:, :], dram["rows"].partition_broadcast(P)).then_inc(sem["loaded"], 16)
            act.dma_start(w["const"][:, :], dram["const"]).then_inc(sem["loaded"], 16)

        @block.vector
        def _(dve):
            dve.memset(w["eps"][:, :], EPS_LN)
            for b in range(4):
                dve.memset(w["values"][b][:, :], 1.0)
            for j in range(NJ + 1):
                if j < NJ:
                    dve.wait_ge(sem[f"x_loaded{j % 4}"], 16 * (j // 4 + 1))
                    for s in range(S):
                        g = s * NJ + j
                        dve.bn_stats(stats[:, g * 6:(g + 1) * 6], x_all[:, s, j, :]).then_inc(sem["stats"], 1)
                if j > 0:
                    dve.wait_ge(sem["stats"], S * j)
                for s in range(S if j > 0 else 0):
                    g = s * NJ + j - 1
                    dve.bn_aggr(w["moments"][:, g * 2:(g + 1) * 2], stats[:, g * 6:(g + 1) * 6])\
                       .then_inc(sem["moments"], 1)
            dve.wait_ge(sem["loaded"], 16 * EARLY)
            dve.tensor_copy(w["before16"][:, :], c["before"])
            dve.tensor_copy(w["ones16"][:, :], c["ones"])
            dve.tensor_scalar(w["g2h"][:, :], w["g2"][:, :], 0.5, None, ALU.mult)
            dve.tensor_scalar(w["be2h"][:, :], w["be2"][:, :], 0.5, None, ALU.mult)


def deviations(nc, w, sem, act, moments, std):
    act.activation(std, moments[:, :].rearrange("p (g two) -> p g two", two=2)[:, :, 1], ACT.Sqrt,
                   bias=w["eps"][:, :]).then_inc(sem["std"], 1)


def attention_phase(nc, c, w, dram, tag, late):
    SB = S * P
    with ExitStack() as ctx:
        def sb(name, shape, dt=F32):
            return ctx.enter_context(nc.sbuf_tensor(f"{tag}_{name}", shape, dt))

        def two(name, shape, dt=F32):
            return [sb(f"{name}_{b}", shape, dt) for b in range(2)]

        def bank(name):
            return ctx.enter_context(nc.psum_tensor(f"{tag}_{name}", [P, 512], F32))

        sem = Names(nc, ctx, tag, "std rstd nmr n nb xb xb_stored*2 late nT nT_sb q k v q_sb k_sb v_sb products "
                    "scores top shifted exps sums inv att weighted paired o oT oT_sb proj r stats1 moments1 kept")
        x_all, res_all = [w[name][:, :].rearrange("p (s j d) -> p s j d", s=S, d=D) for name in ["x", "res"]]

        def block_of(tensor, j):
            return tensor[:, :, bass.ds(j, 1), :].rearrange("p s one d -> p s (one d)")

        xb = two("xb", [P, S, D])
        n, nT, qT, kT, v = [two(name, [P, SB]) for name in ["n", "nT", "qT", "kT", "v"]]
        prod, weighted, paired = [sb(name, [P, width]) for name, width in
                                  [("prod", S * S * P), ("weighted", S * S * P), ("paired", S * S * P // 2)]]
        o, oT = sb("o", [P, SB]), sb("oT", [P, SB])
        std, rstd, nmr = sb("std", [P, NT]), sb("rstd", [P, NT]), sb("nmr", [P, NT])
        stats1, moments1 = sb("stats1", [P, S, 6]), sb("moments1", [P, S, 2])
        top, shifted, exps = sb("top", [P, S * H1]), sb("shifted", [P, PAIRS]), sb("exps", [P, PAIRS])
        sums, inv, att = sb("sums", [P, S * H1]), sb("inv", [P, S * H1]), sb("att", [P, PAIRS])
        pT, pq, pk, pv, pS, pO, pW = [bank(f"bank{i}") for i in range(7)]
        ident = c["ident"]
        xb_v = dram["yx"].rearrange("(s l) d -> l s d", s=S)[:, :, D:2 * D]
        kept = w["moments1"][:, :].rearrange("p (s j two) -> p s j two", s=S, two=2)
        by_s = "p (s d) -> p s d"
        block = ctx.enter_context(nc.Block())

        @block.sync
        def _(sp):
            def store(j, u, r):
                sp.wait_ge(sem["xb"], j + 1)
                sp.dma_start(xb_v[bass.ds(j * P, P), :, :], xb[u][:, :, :]).then_inc(sem[f"xb_stored{u}"], 16)

            for here, there in late:
                sp.dma_start(here, there).then_inc(sem["late"], 16)
            pipeline(sp, [(store, 2)], NJ, 2, 4)
            for u in range(2):
                sp.wait_ge(sem[f"xb_stored{u}"], 16 * (NJ // 2))
            if late:
                sp.wait_ge(sem["late"], 16 * len(late))

        @block.gpsimd
        def _(pool):
            def with_bias(j, u, r):
                pool.wait_ge(sem["n"], S * (j + 1))
                apart(pool)
                pool.tensor_tensor(block_of(res_all, j), n[u][:, :].rearrange(by_s, s=S),
                                   bcast_mid(w["bo"][:, :], S), ALU.add).then_inc(sem["nb"], 1)
                after(pool, sem[f"xb_stored{u}"], 16 * r)
                apart(pool)
                pool.tensor_tensor(xb[u][:, :, :], block_of(x_all, j), bcast_mid(w["be2h"][:, :], S), ALU.add)\
                    .then_inc(sem["xb"], 1)

            def total(j, u, r):
                half = S * P // 2
                after(pool, sem["o"], j)
                apart(pool)
                for s in range(S):
                    pool.wait_ge(sem["weighted"], S * j + s + 1)
                    pool.tensor_tensor(paired[:, s * half:(s + 1) * half], weighted[:, s * SB:s * SB + half],
                                       weighted[:, s * SB + half:(s + 1) * SB], ALU.add).then_inc(sem["paired"], 1)
                pool.wait_ge(sem["paired"], S * (j + 1))
                after(pool, sem["oT"], j)
                two_t = paired[:, :].rearrange("p (s two d) -> p s two d", s=S, two=2)
                pool.tensor_tensor(o[:, :].rearrange(by_s, s=S), two_t[:, :, 0, :], two_t[:, :, 1, :], ALU.add)\
                    .then_inc(sem["o"], 1)

            pipeline(pool, [(with_bias, 1), (total, 2)], NJ, 2, 4)

        @block.vector
        def _(dve):
            dve.wait_ge(sem["std"], 1)
            dve.reciprocal(rstd[:, :], std[:, :]).then_inc(sem["rstd"], 1)
            dve.wait_ge(sem["rstd"], 1)
            dve.scalar_tensor_tensor(nmr[:, :], w["moments"][:, :].rearrange("p (g two) -> p g two", two=2)[:, :, 0],
                                     -1.0, rstd[:, :], ALU.mult, ALU.mult).then_inc(sem["nmr"], 1)

            def products(j, u, r):
                dve.wait_ge(sem["q_sb"], j + 1)
                dve.wait_ge(sem["k_sb"], j + 1)
                after(dve, sem["scores"], j)
                for s in range(S):
                    dve.tensor_tensor(prod[:, s * SB:(s + 1) * SB].rearrange("p (t b) -> p t b", t=S),
                                      bcast_mid(qT[u][:, s * P:(s + 1) * P], S),
                                      kT[u][:, :].rearrange("p (t b) -> p t b", t=S), ALU.mult)\
                       .then_inc(sem["products"], 1)

            def shift(j, u, r):
                dve.wait_ge(sem["scores"], j + 1)
                by_t = pS[:, 0:PAIRS].rearrange("p (s t h) -> p s h t", s=S, t=S)
                dve.tensor_reduce(top[:, :].rearrange("p (s h) -> p s h", s=S), by_t, AX.X, ALU.max)\
                   .then_inc(sem["top"], 1)
                dve.wait_ge(sem["top"], j + 1)
                after(dve, sem["exps"], j)
                dve.tensor_tensor(shifted[:, :].rearrange("p (s t h) -> p s t h", s=S, t=S),
                                  pS[:, 0:PAIRS].rearrange("p (s t h) -> p s t h", s=S, t=S),
                                  top[:, :].rearrange("p (s h) -> p s h", s=S).unsqueeze(2)
                                  .to_broadcast([P, S, S, H1]), ALU.subtract).then_inc(sem["shifted"], 1)

            def weigh(j, u, r):
                dve.wait_ge(sem["exps"], j + 1)
                dve.tensor_reduce(sums[:, :].rearrange("p (s h) -> p s h", s=S),
                                  exps[:, :].rearrange("p (s t h) -> p s h t", s=S, t=S), AX.X, ALU.add)\
                   .then_inc(sem["sums"], 1)
                dve.wait_ge(sem["sums"], j + 1)
                dve.reciprocal(inv[:, :], sums[:, :]).then_inc(sem["inv"], 1)
                dve.wait_ge(sem["inv"], j + 1)
                dve.tensor_tensor(att[:, :].rearrange("p (s t h) -> p s t h", s=S, t=S),
                                  exps[:, :].rearrange("p (s t h) -> p s t h", s=S, t=S),
                                  inv[:, :].rearrange("p (s h) -> p s h", s=S).unsqueeze(2)
                                  .to_broadcast([P, S, S, H1]), ALU.mult).then_inc(sem["att"], 1)
                dve.wait_ge(sem["att"], j + 1)
                dve.wait_ge(sem["v_sb"], j + 1)
                after(dve, sem["paired"], S * j)
                for s in range(S):
                    dve.tensor_tensor(
                        weighted[:, s * SB:(s + 1) * SB].rearrange("p (g d) -> p g d", d=HD1),
                        bcast_last(att[:, s * S * H1:(s + 1) * S * H1], HD1),
                        v[u][:, :].rearrange("p (g d) -> p g d", d=HD1), ALU.mult).then_inc(sem["weighted"], 1)

            def residual(j, u, r):
                dve.wait_ge(sem["proj"], j + 1)
                dve.wait_ge(sem["nb"], j + 1)
                apart(dve)
                here = block_of(res_all, j)
                dve.tensor_tensor(here, pW[:, :].rearrange(by_s, s=S), here, ALU.add).then_inc(sem["r"], 1)
                dve.wait_ge(sem["r"], j + 1)
                apart(dve)
                for s in range(S):
                    dve.bn_stats(stats1[:, s, :], here[:, s, :]).then_inc(sem["stats1"], 1)
                dve.wait_ge(sem["stats1"], S * (j + 1))
                apart(dve)
                for s in range(S):
                    dve.bn_aggr(moments1[:, s, :], stats1[:, s, :]).then_inc(sem["moments1"], 1)
                dve.wait_ge(sem["moments1"], S * (j + 1))
                dve.tensor_copy(kept[:, :, bass.ds(j, 1), :].rearrange("p s one two -> p s (one two)"),
                                moments1[:, :, :]).then_inc(sem["kept"], 1)
                dve.wait_ge(sem["kept"], j + 1)

            pipeline(dve, [(products, 2), (residual, 4), (shift, 2), (weigh, 2)], NJ, 2, 4)

        @block.scalar
        def _(act):
            deviations(nc, w, sem, act, w["moments"], std[:, :])
            act.wait_ge(sem["nmr"], 1)

            def normalise(j, u, r):
                after(act, sem["nT"], j - 1)
                after(act, sem["nb"], j - 1)
                for s in range(S):
                    g = j + s * NJ
                    act.activation(n[u][:, s * D:(s + 1) * D], block_of(x_all, j)[:, s, :], ACT.Identity,
                                   bias=nmr[:, bass.ds(g, 1)], scale=rstd[:, bass.ds(g, 1)]).then_inc(sem["n"], 1)

            def exponent(j, u, r):
                act.wait_ge(sem["shifted"], j + 1)
                after(act, sem["att"], j)
                act.activation(exps[:, :], shifted[:, :], ACT.Exp, scale=HD1 ** -0.5).then_inc(sem["exps"], 1)

            def turned(j, u, r):
                act.wait_ge(sem["nT"], j + 1)
                after(act, sem["v"], j - 1)
                act.activation(nT[u][:, :], pT[:, :], ACT.Copy).then_inc(sem["nT_sb"], 1)

            def project(j, u, r):
                act.wait_ge(sem["q"], j + 1)
                after(act, sem["products"], S * (j - 1))
                act.activation(qT[u][:, :], pq[:, :], ACT.Identity, bias=w["bqkv"][:, 0:1]).then_inc(sem["q_sb"], 1)
                act.wait_ge(sem["k"], j + 1)
                act.activation(kT[u][:, :], pk[:, :], ACT.Identity, bias=w["bqkv"][:, 1:2]).then_inc(sem["k_sb"], 1)
                act.wait_ge(sem["v"], j + 1)
                after(act, sem["weighted"], S * (j - 1))
                act.activation(v[u][:, :], pv[:, :], ACT.Copy).then_inc(sem["v_sb"], 1)

            def outputs(j, u, r):
                act.wait_ge(sem["oT"], j + 1)
                after(act, sem["proj"], j)
                act.activation(oT[:, :], pO[:, :], ACT.Identity, bias=w["bqkv"][:, 2:3]).then_inc(sem["oT_sb"], 1)

            pipeline(act, [(turned, 1), (exponent, 2), (outputs, 3), (project, 1), (normalise, 0)], NJ, 2, 4)

        @block.tensor
        def _(pe):
            def scores(j, u, r):
                after(pe, sem["shifted"], j)
                for s in range(S):
                    pe.wait_ge(sem["products"], S * j + s + 1)
                    for t in range(S):
                        g = s * S + t
                        last = pe.matmul(pS[:, g * H1:(g + 1) * H1], prod[:, g * P:(g + 1) * P], c["heads"],
                                         start=True, stop=True)
                last.then_inc(sem["scores"], 1)

            def turn(j, u, r):
                pe.wait_ge(sem["n"], S * (j + 1))
                after(pe, sem["nT_sb"], j)
                for s in range(S):
                    last = pe.transpose(pT[:, s * P:(s + 1) * P], n[u][:, s * D:(s + 1) * D], ident)
                last.then_inc(sem["nT"], 1)

            def project(j, u, r):
                pe.wait_ge(sem["nT_sb"], j + 1)
                after(pe, sem["q_sb"], j)
                pe.matmul(pq[:, :], w["wqkv"][:, 0:D], nT[u][:, :], start=True, stop=True).then_inc(sem["q"], 1)
                after(pe, sem["k_sb"], j)
                pe.matmul(pk[:, :], w["wqkv"][:, D:2 * D], nT[u][:, :], start=True, stop=True).then_inc(sem["k"], 1)
                after(pe, sem["v_sb"], j)
                for s in range(S):
                    last = pe.matmul(pv[:, s * D:(s + 1) * D], nT[u][:, s * P:(s + 1) * P],
                                     w["wqkv"][:, 2 * D:3 * D], start=True, stop=True)
                last.then_inc(sem["v"], 1)

            def attended(j, u, r):
                pe.wait_ge(sem["o"], j + 1)
                after(pe, sem["oT_sb"], j)
                for s in range(S):
                    last = pe.transpose(pO[:, s * P:(s + 1) * P], o[:, s * P:(s + 1) * P], ident)
                last.then_inc(sem["oT"], 1)

            def combine(j, u, r):
                pe.wait_ge(sem["oT_sb"], j + 1)
                after(pe, sem["r"], j)
                for s in range(S):
                    last = pe.matmul(pW[:, s * D:(s + 1) * D], oT[:, s * P:(s + 1) * P], w["wo"][:, :],
                                     start=True, stop=True)
                last.then_inc(sem["proj"], 1)

            pipeline(pe, [(scores, 2), (turn, 1), (attended, 3), (project, 1), (combine, 3)], NJ, 2, 4)


def router_phase(nc, c, w, dram, tag):
    SB = S * P
    with ExitStack() as ctx:
        def sb(name, shape, dt=F32):
            return ctx.enter_context(nc.sbuf_tensor(f"{tag}_{name}", shape, dt))

        def some(k, make, name, shape):
            return [make(f"{name}_{b}", shape) for b in range(k)]

        def bank(name, shape):
            return ctx.enter_context(nc.psum_tensor(f"{tag}_bank_{name}", shape, F32))

        sem = Names(nc, ctx, tag, "std rstd nmr zg y z y_last y_stored*4 yT yT_sb logits kept")
        res_all = w["res"][:, :].rearrange("p (s j d) -> p s j d", s=S, d=D)
        std, rstd, nmr = sb("std", [P, NT]), sb("rstd", [P, NT]), sb("nmr", [P, NT])
        z = some(2, sb, "z", [P, D])
        zg, y, yT = sb("zg", [P, SB]), some(4, sb, "y", [P, S, D]), some(2, sb, "yT", [P, SB])
        pY, pL = some(2, bank, "yT", [P, 512]), some(2, bank, "logits", [P, 512])
        y_v = dram["yx"].rearrange("(s l) d -> l s d", s=S)[:, :, 0:D]
        mean = w["moments1"][:, :].rearrange("p (g two) -> p g two", two=2)[:, :, 0]
        block = ctx.enter_context(nc.Block())

        @block.sync
        def _(sp):
            def store(j, u, r):
                sp.wait_ge(sem["y"], (S - 1) * (j + 1))
                sp.wait_ge(sem["y_last"], 2 * (j + 1))
                sp.dma_start(y_v[bass.ds(j * P, P), :, :], y[u][:, :, :]).then_inc(sem[f"y_stored{u}"], 16)

            straight([(store, 0)], NJ, 4)
            for u in range(4):
                sp.wait_ge(sem[f"y_stored{u}"], 16 * (NJ // 4))

        @block.vector
        def _(dve):
            dve.wait_ge(sem["std"], 1)
            dve.reciprocal(rstd[:, :], std[:, :]).then_inc(sem["rstd"], 1)
            dve.wait_ge(sem["rstd"], 1)
            dve.scalar_tensor_tensor(nmr[:, :], mean, -1.0, rstd[:, :], ALU.mult, ALU.mult).then_inc(sem["nmr"], 1)

            def affine(j, u, r):
                after(dve, sem["y"], (S - 1) * j)
                for s in range(S - 1):
                    dve.scalar_tensor_tensor(zg[:, s * D:(s + 1) * D],
                                             res_all[:, s, j, :],
                                             mean[:, j + s * NJ:j + s * NJ + 1], w["g1"][:, :],
                                             ALU.subtract, ALU.mult).then_inc(sem["zg"], 1)
                dve.wait_ge(sem["zg"], (S - 1) * (j + 1))
                after(dve, sem["yT"], j - 3)
                after(dve, sem[f"y_stored{u}"], 16 * r)
                for s in range(S - 1):
                    dve.scalar_tensor_tensor(y[u][:, s, :], zg[:, s * D:(s + 1) * D],
                                             rstd[:, j + s * NJ:j + s * NJ + 1], w["be1"][:, :],
                                             ALU.mult, ALU.add).then_inc(sem["y"], 1)

            straight([(affine, 0)], NJ, 4)

        @block.gpsimd
        def _(pool):
            def affine(j, u, r):
                pool.wait_ge(sem["z"], j + 1)
                after(pool, sem["yT"], j - 3)
                after(pool, sem[f"y_stored{u}"], 16 * r)
                pool.tensor_tensor(y[u][:, S - 1, :], z[u % 2][:, :], w["g1"][:, :], ALU.mult)\
                    .then_inc(sem["y_last"], 1)
                pool.wait_ge(sem["y_last"], 2 * j + 1)
                pool.tensor_tensor(y[u][:, S - 1, :], y[u][:, S - 1, :], w["be1"][:, :], ALU.add)\
                    .then_inc(sem["y_last"], 1)

            straight([(affine, 0)], NJ, 4)

        @block.scalar
        def _(act):
            deviations(nc, w, sem, act, w["moments1"], std[:, :])

            def centre(j, u, r):
                after(act, sem["y_last"], 2 * (j - 1))
                g = (S - 1) * NJ + j
                act.activation(z[u % 2][:, :], res_all[:, S - 1, j, :], ACT.Identity, bias=nmr[:, g:g + 1],
                               scale=rstd[:, g:g + 1]).then_inc(sem["z"], 1)

            def turned(j, u, r):
                act.wait_ge(sem["yT"], j + 1)
                after(act, sem["logits"], j - 1)
                act.activation(yT[u % 2][:, :], pY[u % 2][:, :], ACT.Copy).then_inc(sem["yT_sb"], 1)

            def keep(j, u, r):
                act.wait_ge(sem["logits"], j + 1)
                act.activation(w["logits"][:, bass.ds(j * S * E, S * E)], pL[u % 2][:, 0:S * E], ACT.Copy)\
                   .then_inc(sem["kept"], 1)

            act.wait_ge(sem["nmr"], 1)
            straight([(centre, 0), (turned, 1), (keep, 2)], NJ, 4)

        @block.tensor
        def _(pe):
            def turn(j, u, r):
                after(pe, sem["yT_sb"], j - 1)
                for s in range(S):
                    if s < S - 1:
                        pe.wait_ge(sem["y"], (S - 1) * j + s + 1)
                    else:
                        pe.wait_ge(sem["y_last"], 2 * (j + 1))
                    last = pe.transpose(pY[u % 2][:, s * P:(s + 1) * P], y[u][:, s, :], c["ident"])
                last.then_inc(sem["yT"], 1)

            def router(j, u, r):
                pe.wait_ge(sem["yT_sb"], j + 1)
                after(pe, sem["kept"], j - 1)
                for s in range(S):
                    last = pe.matmul(pL[u % 2][:, s * E:(s + 1) * E], yT[u % 2][:, s * P:(s + 1) * P], w["wg"][:, :],
                                     start=True, stop=True)
                last.then_inc(sem["logits"], 1)

            straight([(turn, 0), (router, 1)], NJ, 4)


def routing_phase(nc, c, w, tag):
    EG = E * NT
    with ExitStack() as ctx:
        def sb(name, shape, dt=F32):
            return ctx.enter_context(nc.sbuf_tensor(f"{tag}_{name}", shape, dt))

        sem = Names(nc, ctx, tag, "dve prefix high_marks inverse")
        best, tied, first = sb("best", [P, NT]), sb("tied", [P, EG]), sb("first", [P, NT])
        chosen16 = sb("chosen16", [P, EG], BF16)
        summed, zeros = sb("summed", [P, EG]), sb("zeros", [P, EG])
        counts, full, tiles = sb("counts", [P, E]), sb("full", [P, EG]), sb("tiles", [P, E])
        ends, shift = sb("ends", [P, E]), sb("shift", [P, E])
        slot, where = sb("slot_of", [P, EG]), sb("where", [P, NT])
        where_i, tile_i, lane_i = sb("where_i", [P, NT], I32), sb("tile_i", [P, NT], I32), sb("lane_i", [P, NT], I32)
        tile_f, lane_f = sb("tile_f", [P, NT]), sb("lane_f", [P, NT])
        passed, expert = sb("passed", [P, SLOTS * (E - 1)]), sb("expert_f", [P, SLOTS])
        lanes = sb("lanes", [P, NT * P], BF16)
        marks = sb("marks", [P, NT * 3 * SLOTS], BF16)
        low, reads, empty = sb("low", [P, SLOTS]), sb("reads_f", [P, SLOTS]), sb("empty", [P, SLOTS])
        pR = ctx.enter_context(nc.psum_tensor(f"{tag}_pPrefix", [P, 512], F32))
        pI = ctx.enter_context(nc.psum_tensor(f"{tag}_pInverse", [P, 512], F32))
        by_e = "p (e g) -> p e g"
        count_at = {}
        marks_v = marks[:, :].rearrange("p (g k t) -> p g k t", g=NT, k=3)
        block = ctx.enter_context(nc.Block())

        @block.vector
        def _(dve):
            done = [0]

            def count(instruction):
                done[0] += 1
                instruction.then_inc(sem["dve"], 1)

            def then(instruction):
                count(instruction)
                dve.wait_ge(sem["dve"], done[0])

            logits = w["logits"][:, :].rearrange("p (g e) -> p g e", e=E)
            tied_v = tied[:, :].rearrange("p (g e) -> p g e", e=E)
            then(dve.tensor_reduce(best[:, :], logits, AX.X, ALU.max))
            then(dve.tensor_tensor(tied_v, logits, bcast_last(best[:, :], E), ALU.is_ge))
            then(dve.tensor_tensor(tied_v, tied_v, bcast_mid(c["rank"], NT), ALU.mult))
            then(dve.tensor_reduce(first[:, :], tied_v, AX.X, ALU.max))
            then(dve.tensor_tensor(chosen16[:, :].rearrange("p (e g) -> p g e", e=E),
                                   bcast_mid(c["rank"], NT), bcast_last(first[:, :], E), ALU.is_equal))
            count_at["chosen"] = done[0]
            count(dve.memset(zeros[:, :], 0.0))
            totals = pR[:, EG:2 * EG]
            dve.wait_ge(sem["prefix"], 1)
            then(dve.tensor_reduce(counts[:, :], totals.rearrange(by_e, e=E), AX.X, ALU.add))
            count(dve.tensor_tensor_scan(summed[:, :], totals, zeros[:, :], 0.0, ALU.add, ALU.add))
            then(dve.tensor_tensor(full[:, :].rearrange(by_e, e=E), bcast_last(counts[:, :], NT),
                                   bcast_mid(c["filled"], E), ALU.is_gt))
            count(dve.tensor_tensor(summed[:, :], summed[:, :], totals, ALU.subtract))
            then(dve.tensor_reduce(tiles[:, :], full[:, :].rearrange(by_e, e=E), AX.X, ALU.add))
            then(dve.tensor_tensor_scan(ends[:, :], tiles[:, :], zeros[:, 0:E], 0.0, ALU.add, ALU.add))
            count_at["ends"] = done[0]
            then(dve.tensor_tensor(shift[:, :], ends[:, :], tiles[:, :], ALU.subtract))
            count(dve.scalar_tensor_tensor(shift[:, :], shift[:, :], float(P),
                                           summed[:, :].rearrange(by_e, e=E)[:, :, 0], ALU.mult, ALU.subtract))
            then(dve.tensor_tensor(slot[:, :], summed[:, :], pR[:, 0:EG], ALU.add))
            then(dve.tensor_tensor(slot[:, :].rearrange(by_e, e=E), slot[:, :].rearrange(by_e, e=E),
                                   bcast_last(shift[:, :], NT), ALU.add))
            then(dve.tensor_tensor(slot[:, :], slot[:, :], chosen16[:, :], ALU.mult))
            then(dve.tensor_reduce(where[:, :], slot[:, :].rearrange("p (e g) -> p g e", e=E), AX.X, ALU.add))
            then(dve.tensor_copy(where_i[:, :], where[:, :]))
            count(dve.tensor_scalar(tile_i[:, :], where_i[:, :], 7, None, ALU.logical_shift_right))
            then(dve.tensor_scalar(lane_i[:, :], where_i[:, :], P - 1, None, ALU.bitwise_and))
            count(dve.tensor_copy(lane_f[:, :], lane_i[:, :]))
            then(dve.tensor_copy(tile_f[:, :], tile_i[:, :]))
            then(dve.tensor_tensor(marks_v[:, :, 2, :], bcast_mid(c["slot"], NT), bcast_last(tile_f[:, :], SLOTS),
                                   ALU.is_equal))
            count_at["marks"] = done[0]
            count(dve.tensor_scalar(marks_v[:, :, 0, :], marks_v[:, :, 2, :], c["part"], None, ALU.mult))
            for g in range(0, NT, S):
                count(dve.tensor_tensor(lanes[:, g * P:(g + S) * P].rearrange("p (g l) -> p g l", g=S),
                                        bcast_mid(c["lane"], S), bcast_last(lane_f[:, g:g + S], P), ALU.is_equal))
                count_at[g // S] = done[0]
            then(dve.tensor_tensor(passed[:, :].rearrange("p (t e) -> p t e", e=E - 1), bcast_last(c["slot"], E - 1),
                                   bcast_mid(ends[:, 0:E - 1], SLOTS), ALU.is_ge))
            then(dve.tensor_reduce(expert[:, :], passed[:, :].rearrange("p (t e) -> p t e", e=E - 1), AX.X, ALU.add))
            count(dve.tensor_copy(w["expert"][:, :], expert[:, :]))
            dve.wait_ge(sem["inverse"], 1)
            low_p, high_p, used_p = [pI[:, k * SLOTS:(k + 1) * SLOTS] for k in range(3)]
            count(dve.tensor_scalar(empty[:, :], used_p, -1.0, 1.0, ALU.mult, ALU.add))
            then(dve.tensor_copy(low[:, :], low_p))
            count(dve.tensor_tensor(empty[:, :], empty[:, :], c["spare"], ALU.mult))
            then(dve.scalar_tensor_tensor(reads[:, :], high_p, float(P), low[:, :], ALU.mult, ALU.add))
            count(dve.tensor_copy(w["reads"][:, :], reads[:, :]))
            count(dve.tensor_tensor(w["writes"][:, :], reads[:, :], empty[:, :], ALU.add))

        @block.gpsimd
        def _(pool):
            pool.wait_ge(sem["dve"], count_at["marks"])
            pool.tensor_tensor(marks_v[:, :, 1, :], marks_v[:, :, 2, :], bcast_last(c["high"], SLOTS), ALU.mult)\
                .then_inc(sem["high_marks"], 1)

        @block.tensor
        def _(pe):
            pe.wait_ge(sem["dve"], count_at["chosen"])
            pe.matmul(pR[:, 0:EG], w["before16"][:, :], chosen16[:, :], start=True, stop=True)
            pe.matmul(pR[:, EG:2 * EG], w["ones16"][:, :], chosen16[:, :], start=True, stop=True)\
              .then_inc(sem["prefix"], 1)
            pe.wait_ge(sem["high_marks"], 1)
            for g in range(NT):
                if g % S == 0:
                    pe.wait_ge(sem["dve"], count_at[g // S])
                last = pe.matmul(pI[:, 0:3 * SLOTS], lanes[:, g * P:(g + 1) * P],
                                 marks[:, g * 3 * SLOTS:(g + 1) * 3 * SLOTS], start=(g == 0), stop=(g == NT - 1))
            last.then_inc(sem["inverse"], 1)


def experts_phase(nc, c, w, dram, dst, tag):
    FIRST = 16
    with ExitStack() as ctx:
        def sb(name, shape, dt=F32):
            return ctx.enter_context(nc.sbuf_tensor(f"{tag}_{name}", shape, dt))

        def some(k, name, shape, dt=F32):
            return [sb(f"{name}_{b}", shape, dt) for b in range(k)]

        def bank(name):
            return ctx.enter_context(nc.psum_tensor(f"{tag}_{name}", [P, 512], F32))

        sem = Names(nc, ctx, tag, "index gathered*8 w1 yT yT_sb h hb hT o a stats moments std rstd zg out "
                    "out_index scattered*8")
        index, out_index = some(2, "index", [P, 4], I32), some(2, "out_index", [P, 4], I32)
        rows = some(8, "rows", [P, 2 * D])
        out = some(8, "out", [P, D])
        w1 = some(2, "w1", [P, DF])
        yT, hb, hT = some(4, "yT", [P, P]), some(2, "hb", [P, DF]), some(2, "hT", [P, DF])
        a, zg = some(2, "a", [P, D]), sb("zg", [P, D])
        stats, moments, rstd, std = sb("stats", [P, 6]), sb("moments", [P, 2]), sb("rstd", [P, 1]), sb("std", [P, 1])
        pT, pH, pO = bank("turn"), [bank("h0"), bank("h1")], [bank("o0"), bank("o1")]
        ident = c["ident"]
        block = ctx.enter_context(nc.Block())

        @block.gpsimd
        def _(pool):
            def gather(t, u, r):
                if isinstance(t, int):
                    numbers = w["reads"][:, t:t + 1]
                else:
                    pool.wait_ge(sem["index"], 2 * (r - FIRST // 8) + u // 4 + 1)
                    numbers = index[u // 4][:, u % 4:u % 4 + 1]
                after(pool, sem["out"], t - 7)
                apart(pool)
                pool.indirect_dma_start(rows[u][:, :], None, dram["yx"],
                                        bass.IndirectOffsetOnAxis(ap=numbers, axis=0))\
                    .then_inc(sem[f"gathered{u}"], 16)

            def scatter(t, u, r):
                pool.wait_ge(sem["out_index"], 2 * r + u // 4 + 1)
                pool.wait_ge(sem["out"], t + 1)
                apart(pool)
                numbers = out_index[u // 4][:, u % 4:u % 4 + 1]
                pool.indirect_dma_start(dst, bass.IndirectOffsetOnAxis(ap=numbers, axis=0),
                                        out[u][:, :], None).then_inc(sem[f"scattered{u}"], 16)

            pipeline(pool, [(gather, 0), (scatter, 7)], SLOTS, 8, FIRST)
            for u in range(8):
                pool.wait_ge(sem[f"scattered{u}"], 16 * (SLOTS // 8))

        @block.scalar
        def _(act):
            experts = Experts(nc, w, mybir.EngineType.Activation, [2])

            def weights(t, u, r):
                e = experts.of(2)
                after(act, sem["h"], t - 1)
                act.activation(w1[u % 2][:, :], w["w1"][:, bass.ds(e * DF, DF)], ACT.Copy).then_inc(sem["w1"], 1)

            def turned(t, u, r):
                act.wait_ge(sem["yT"], t + 1)
                after(act, sem["o"], t - 3)
                act.activation(yT[u % 4][:, :], pT[:, 0:P], ACT.Copy).then_inc(sem["yT_sb"], 1)

            def relu(t, u, r):
                act.wait_ge(sem["hb"], t + 1)
                after(act, sem["o"], t - 1)
                act.activation(hT[u % 2][:, :], hb[u % 2][:, :], ACT.Relu).then_inc(sem["hT"], 1)

            def deviation(t, u, r):
                act.wait_ge(sem["moments"], t + 1)
                after(act, sem["rstd"], t)
                act.activation(std[:, :], moments[:, 1:2], ACT.Sqrt, bias=w["eps"][:, :]).then_inc(sem["std"], 1)

            pipeline(act, [(relu, 4), (weights, 2), (turned, 2), (deviation, 5)], SLOTS, 8, FIRST, experts)

        @block.tensor
        def _(pe):
            experts = Experts(nc, w, mybir.EngineType.PE, [4])

            def turn(t, u, r):
                pe.wait_ge(sem[f"gathered{u}"], 16 * (r + 1))
                after(pe, sem["yT_sb"], t)
                pe.transpose(pT[:, 0:P], rows[u][:, 0:D], ident).then_inc(sem["yT"], 1)

            def up(t, u, r):
                pe.wait_ge(sem["w1"], t + 1)
                pe.wait_ge(sem["yT_sb"], t + 1)
                after(pe, sem["hb"], t - 1)
                for k in range(NC):
                    last = pe.matmul(pH[u % 2][:, k * P:(k + 1) * P], w1[u % 2][:, k * P:(k + 1) * P],
                                     yT[u % 4][:, :], start=True, stop=True)
                last.then_inc(sem["h"], 1)

            def down(t, u, r):
                e = experts.of(4)
                pe.wait_ge(sem["hT"], t + 1)
                after(pe, sem["a"], t - 1)
                pe.matmul(pO[u % 2][:, 0:D], yT[u % 4][:, :], ident, start=True, stop=False)
                for k in range(NC):
                    last = pe.matmul(pO[u % 2][:, 0:D], hT[u % 2][:, k * P:(k + 1) * P],
                                     w["w2"][:, bass.ds(e * DF + k * D, D)], start=False, stop=(k == NC - 1))
                last.then_inc(sem["o"], 1)

            pipeline(pe, [(up, 3), (turn, 2), (down, 4)], SLOTS, 8, FIRST, experts)

        @block.vector
        def _(dve):
            experts = Experts(nc, w, mybir.EngineType.DVE, [3, 5])

            def bias(t, u, r):
                e = experts.of(3)
                dve.wait_ge(sem["h"], t + 1)
                after(dve, sem["hT"], t - 1)
                dve.tensor_tensor(hb[u % 2][:, :].rearrange("p (k b) -> p k b", k=NC),
                                  pH[u % 2][:, :].rearrange("p (k b) -> p k b", k=NC),
                                  bcast_last(w["b1"][:, bass.ds(e * NC, NC)], P), ALU.add).then_inc(sem["hb"], 1)

            def indices(t, u, r):
                if not isinstance(t, int) and u % 4 == 0:
                    for b in range(u, u + 4):
                        after(dve, sem[f"gathered{b}"], 16 * r)
                    dve.tensor_copy(index[u // 4][:, :], w["reads"][:, bass.ds(t, 4)]).then_inc(sem["index"], 1)

            def out_indices(t, u, r):
                if u % 4 == 0:
                    for b in range(u, u + 4):
                        after(dve, sem[f"scattered{b}"], 16 * r)
                    dve.tensor_copy(out_index[u // 4][:, :], w["writes"][:, bass.ds(t, 4)])\
                       .then_inc(sem["out_index"], 1)

            def add(t, u, r):
                e = experts.of(5)
                dve.wait_ge(sem["o"], t + 1)
                after(dve, sem["zg"], t - 1)
                dve.tensor_tensor(a[u % 2][:, :], pO[u % 2][:, 0:D], w["b2"][:, bass.ds(e * D, D)], ALU.add)\
                   .then_inc(sem["a"], 1)

            def statistics(t, u, r):
                dve.wait_ge(sem["a"], t + 1)
                after(dve, sem["moments"], t)
                apart(dve)
                dve.bn_stats(stats[:, :], a[u % 2][:, :]).then_inc(sem["stats"], 1)

            def aggregate(t, u, r):
                dve.wait_ge(sem["stats"], t + 1)
                after(dve, sem["zg"], t)
                apart(dve)
                dve.bn_aggr(moments[:, :], stats[:, :]).then_inc(sem["moments"], 1)

            def centre(t, u, r):
                dve.wait_ge(sem["moments"], t + 1)
                after(dve, sem["out"], t)
                dve.scalar_tensor_tensor(zg[:, :], a[u % 2][:, :], moments[:, 0:1], w["g2h"][:, :],
                                         ALU.subtract, ALU.mult).then_inc(sem["zg"], 1)

            def inverse(t, u, r):
                dve.wait_ge(sem["std"], t + 1)
                after(dve, sem["out"], t)
                dve.reciprocal(rstd[:, :], std[:, :]).then_inc(sem["rstd"], 1)

            def finish(t, u, r):
                dve.wait_ge(sem["rstd"], t + 1)
                dve.wait_ge(sem["zg"], t + 1)
                after(dve, sem[f"scattered{u}"], 16 * r)
                dve.scalar_tensor_tensor(out[u][:, :], zg[:, :], rstd[:, 0:1], rows[u][:, D:2 * D],
                                         ALU.mult, ALU.add).then_inc(sem["out"], 1)

            pipeline(dve, [(centre, 6), (add, 5), (inverse, 6), (indices, 0), (finish, 6), (out_indices, 6),
                           (statistics, 5), (bias, 3), (aggregate, 5)], SLOTS, 8, FIRST, experts)


def linear_attention_phase(nc, c, w, src, tag):
    QK = 2 * D
    KV = H2 * HM * HD2
    PIECES = [(0, 6), (6, 11), (11, 16)]
    LOADED = 4
    with ExitStack() as ctx:
        def sb(name, shape, dt=F32):
            return ctx.enter_context(nc.sbuf_tensor(f"{tag}_{name}", shape, dt))

        def some(k, name, shape, dt=F32):
            return [sb(f"{name}_{b}", shape, dt) for b in range(k)]

        def bank(name):
            return ctx.enter_context(nc.psum_tensor(f"{tag}_bank_{name}", [P, 512], F32))

        sem = Names(nc, ctx, tag, "x_loaded stats moments std rstd n nT nT_sb qkv qk_sb v_sb rc rs rot relu "
                    "kv cum prod num den inv o oT oT_sb proj out stats2 moments2 kept")
        x = w["x"]
        n = some(2, "n", [P, D])
        stats, moments, rstd, std = sb("stats", [P, 6]), sb("moments", [P, 2]), sb("rstd", [P, 1]), sb("std", [P, 1])
        stats2, moments2 = sb("stats2", [P, 6]), sb("moments2", [P, 2])
        nT = sb("nT", [P, P])
        qk, rc, rs, rot = some(2, "qk", [P, QK]), sb("rc", [P, QK]), sb("rs", [P, QK]), sb("rot", [P, QK])
        relu = some(4, "relu", [P, QK])
        values = w["values"]
        kv, prod = some(4, "kv", [P, KV]), sb("prod", [P, KV])
        num, den, inv = sb("num", [P, H2 * HM]), sb("den", [P, H2]), sb("inv", [P, H2])
        o, oT = some(4, "o", [P, D]), sb("oT", [P, P])
        pN, pQ, pT, pO, pA, pB, pC = [bank(name) for name in ["nT", "qkv", "oT", "proj", "sumA", "sumB", "sumC"]]
        pieces = [pA, pB, pC]
        ident = c["ident"]
        hm = "p (h m) -> p h m"
        block = ctx.enter_context(nc.Block())

        @block.sync
        def _(sp):
            for g in range(NT // LOADED):
                sp.dma_start(x[:, g * LOADED * D:(g + 1) * LOADED * D].rearrange("p (t d) -> p t d", d=D),
                             src[g * LOADED * P:(g + 1) * LOADED * P, :].rearrange("(t p) d -> p t d", p=P))\
                  .then_inc(sem["x_loaded"], 16)
                sp.wait_ge(sem["x_loaded"], 16 * (g + 1))

        @block.vector
        def _(dve):
            def statistics(t, u, r):
                if isinstance(t, int):
                    loaded = 16 * (t // LOADED + 1)
                else:
                    loaded = 16 * (r * (NJ // LOADED) + u // LOADED + 1)
                dve.wait_ge(sem["x_loaded"], loaded)
                apart(dve)
                after(dve, sem["moments"], t)
                dve.bn_stats(stats[:, :], x[:, bass.ds(t * D, D)]).then_inc(sem["stats"], 1)

            def aggregate(t, u, r):
                dve.wait_ge(sem["stats"], t + 1)
                after(dve, sem["n"], t)
                apart(dve)
                dve.bn_aggr(moments[:, :], stats[:, :]).then_inc(sem["moments"], 1)

            def inverse(t, u, r):
                dve.wait_ge(sem["std"], t + 1)
                after(dve, sem["n"], t)
                dve.reciprocal(rstd[:, :], std[:, :]).then_inc(sem["rstd"], 1)

            def normalise(t, u, r):
                dve.wait_ge(sem["rstd"], t + 1)
                after(dve, sem["nT"], t - 1)
                dve.tensor_scalar(n[u % 2][:, :], x[:, bass.ds(t * D, D)], moments[:, 0:1], rstd[:, 0:1],
                                  ALU.subtract, ALU.mult).then_inc(sem["n"], 1)

            def multiply(k):
                def piece(t, u, r):
                    h0, h1 = PIECES[k]
                    dve.wait_ge(sem["cum"], 3 * t + k + 1)
                    after(dve, sem["num"], t)
                    q = relu[u % 4][:, h0 * HD2:h1 * HD2].rearrange("p (h d) -> p h d", d=HD2)
                    size = [P, h1 - h0, HM, HD2]
                    dve.tensor_tensor(
                        prod[:, h0 * HM * HD2:h1 * HM * HD2].rearrange("p (h m d) -> p h m d", m=HM, d=HD2),
                        pieces[k][:, 0:(h1 - h0) * HM * HD2].rearrange("p (h m d) -> p h m d", m=HM, d=HD2),
                        q.unsqueeze(2).to_broadcast(size), ALU.mult).then_inc(sem["prod"], 1)
                return piece

            def total(t, u, r):
                dve.wait_ge(sem["prod"], 3 * (t + 1))
                after(dve, sem["o"], t)
                dve.tensor_reduce(num[:, :], prod[:, :].rearrange("p (g d) -> p g d", d=HD2), AX.X, ALU.add)\
                   .then_inc(sem["num"], 1)

            def denominator(t, u, r):
                dve.wait_ge(sem["num"], t + 1)
                after(dve, sem["inv"], t)
                dve.tensor_scalar(den[:, :], num[:, :].rearrange(hm, m=HM)[:, :, HD2], EPS_LA, None, ALU.add)\
                   .then_inc(sem["den"], 1)

            def invert(t, u, r):
                dve.wait_ge(sem["den"], t + 1)
                after(dve, sem["o"], t)
                dve.reciprocal(inv[:, :], den[:, :]).then_inc(sem["inv"], 1)

            def divide(t, u, r):
                dve.wait_ge(sem["inv"], t + 1)
                after(dve, sem["oT"], t - 2)
                dve.tensor_tensor(o[u % 4][:, :].rearrange("p (h m) -> p h m", m=HD2),
                                  num[:, :].rearrange(hm, m=HM)[:, :, 0:HD2],
                                  bcast_last(inv[:, :], HD2), ALU.mult).then_inc(sem["o"], 1)

            def finish(t, u, r):
                dve.wait_ge(sem["proj"], t + 1)
                apart(dve)
                here = x[:, bass.ds(t * D, D)]
                dve.tensor_tensor(here, pO[:, 0:D], here, ALU.add).then_inc(sem["out"], 1)

            def statistics2(t, u, r):
                dve.wait_ge(sem["out"], t + 1)
                after(dve, sem["moments2"], t)
                apart(dve)
                dve.bn_stats(stats2[:, :], x[:, bass.ds(t * D, D)]).then_inc(sem["stats2"], 1)

            def aggregate2(t, u, r):
                dve.wait_ge(sem["stats2"], t + 1)
                after(dve, sem["kept"], t)
                apart(dve)
                dve.bn_aggr(moments2[:, :], stats2[:, :]).then_inc(sem["moments2"], 1)

            def keep(t, u, r):
                dve.wait_ge(sem["moments2"], t + 1)
                dve.tensor_copy(w["moments"][:, bass.ds(2 * t, 2)], moments2[:, :]).then_inc(sem["kept"], 1)

            pipeline(dve, [(finish, 7), (denominator, 5), (statistics, 0), (invert, 5), (multiply(0), 4), (divide, 5),
                           (aggregate, 0), (statistics2, 7), (multiply(1), 4), (aggregate2, 7), (inverse, 0),
                           (multiply(2), 4), (keep, 7), (normalise, 0), (total, 4)], NT, 8, 8)

        @block.gpsimd
        def _(pool):
            def rotate(t, u, r):
                pool.wait_ge(sem["qk_sb"], t + 1)
                after(pool, sem["rot"], t)
                heads = [P, 2 * H2, HD2]
                cos = bcast_mid(c["cos"][:, u * HD2:(u + 1) * HD2], 2 * H2)
                sin = c["sin"][:, u * HD2:(u + 1) * HD2].rearrange("p (i two) -> p i two", two=2)
                pairs = "p (h i two) -> p h i two"
                pool.tensor_tensor(rc[:, :].rearrange("p (h d) -> p h d", d=HD2),
                                   qk[u % 2][:, :].rearrange("p (h d) -> p h d", d=HD2), cos, ALU.mult)\
                    .then_inc(sem["rc"], 1)
                for side in range(2):
                    pool.tensor_tensor(rs[:, :].rearrange(pairs, i=HD2 // 2, two=2)[:, :, :, side],
                                       qk[u % 2][:, :].rearrange(pairs, i=HD2 // 2, two=2)[:, :, :, 1 - side],
                                       bcast_mid(sin[:, :, side], 2 * H2), ALU.mult).then_inc(sem["rs"], 1)
                pool.wait_ge(sem["rc"], t + 1)
                pool.wait_ge(sem["rs"], 2 * (t + 1))
                after(pool, sem["relu"], t)
                pool.tensor_tensor(rot[:, :], rc[:, :], rs[:, :], ALU.add).then_inc(sem["rot"], 1)

            def outer(t, u, r):
                pool.wait_ge(sem["relu"], t + 1)
                pool.wait_ge(sem["v_sb"], t + 1)
                after(pool, sem["cum"], 3 * (t - 2))
                size = [P, H2, HM, HD2]
                k = relu[u % 4][:, D:QK].rearrange("p (h d) -> p h d", d=HD2)
                pool.tensor_tensor(kv[u % 4][:, :].rearrange("p (h m d) -> p h m d", m=HM, d=HD2),
                                   k.unsqueeze(2).to_broadcast(size),
                                   bcast_last(values[u % 4][:, :].rearrange(hm, m=HM), HD2), ALU.mult)\
                    .then_inc(sem["kv"], 1)

            pipeline(pool, [(rotate, 2), (outer, 3)], NT, 8, 8)

        @block.scalar
        def _(act):
            def turned(t, u, r):
                act.wait_ge(sem["nT"], t + 1)
                after(act, sem["qkv"], t)
                act.activation(nT[:, :], pN[:, 0:P], ACT.Copy).then_inc(sem["nT_sb"], 1)

            def project(t, u, r):
                act.wait_ge(sem["qkv"], t + 1)
                after(act, sem["rc"], t - 1)
                after(act, sem["rs"], 2 * (t - 1))
                act.activation(qk[u % 2][:, :], pQ[:, 0:QK], ACT.Copy).then_inc(sem["qk_sb"], 1)
                after(act, sem["kv"], t - 3)
                act.activation(values[u % 4][:, :].rearrange(hm, m=HM)[:, :, 0:HD2],
                               pQ[:, QK:QK + D].rearrange("p (h m) -> p h m", m=HD2), ACT.Copy)\
                   .then_inc(sem["v_sb"], 1)

            def rectify(t, u, r):
                act.wait_ge(sem["rot"], t + 1)
                after(act, sem["kv"], t - 3)
                after(act, sem["prod"], 3 * (t - 3))
                act.activation(relu[u % 4][:, :], rot[:, :], ACT.Relu).then_inc(sem["relu"], 1)

            def outputs(t, u, r):
                act.wait_ge(sem["oT"], t + 1)
                after(act, sem["proj"], t)
                act.activation(oT[:, :], pT[:, 0:P], ACT.Copy).then_inc(sem["oT_sb"], 1)

            def deviation(t, u, r):
                act.wait_ge(sem["moments"], t + 1)
                after(act, sem["rstd"], t)
                act.activation(std[:, :], moments[:, 1:2], ACT.Sqrt, bias=w["eps"][:, :]).then_inc(sem["std"], 1)

            pipeline(act, [(turned, 1), (outputs, 6), (deviation, 0), (project, 1), (rectify, 2)], NT, 8, 8)

        @block.tensor
        def _(pe):
            def turn(t, u, r):
                pe.wait_ge(sem["n"], t + 1)
                after(pe, sem["nT_sb"], t)
                pe.transpose(pN[:, 0:P], n[u % 2][:, :], ident).then_inc(sem["nT"], 1)

            def running(k):
                def piece(t, u, r):
                    h0, h1 = PIECES[k]
                    columns = slice(h0 * HM * HD2, h1 * HM * HD2)
                    size = (h1 - h0) * HM * HD2
                    after(pe, sem["prod"], 3 * (t - 1) + k + 1)
                    if u > 0:
                        pe.matmul(pieces[k][:, 0:size], c["later"], kv[(u - 1) % 4][:, columns],
                                  start=False, stop=False, skip_group_check=True)
                    pe.wait_ge(sem["kv"], t + 1)
                    pe.matmul(pieces[k][:, 0:size], c["upto"], kv[u % 4][:, columns],
                              start=(u == 0), stop=True, skip_group_check=True).then_inc(sem["cum"], 1)
                return piece

            def project(t, u, r):
                pe.wait_ge(sem["nT_sb"], t + 1)
                after(pe, sem["v_sb"], t)
                pe.matmul(pQ[:, 0:3 * D], nT[:, :], w["la_wqkv"][:, :], start=True, stop=True)\
                  .then_inc(sem["qkv"], 1)

            def output(t, u, r):
                pe.wait_ge(sem["o"], t + 1)
                after(pe, sem["oT_sb"], t)
                pe.transpose(pT[:, 0:P], o[u % 4][:, :], ident).then_inc(sem["oT"], 1)

            def combine(t, u, r):
                pe.wait_ge(sem["oT_sb"], t + 1)
                after(pe, sem["out"], t)
                pe.matmul(pO[:, 0:D], oT[:, :], w["la_wo"][:, :], start=True, stop=True)\
                  .then_inc(sem["proj"], 1)

            pipeline(pe, [(running(0), 4), (turn, 1), (running(1), 4), (project, 1), (output, 6), (running(2), 4),
                          (combine, 6)], NT, 8, 8)


def macaron_kernel(nc, dram, out):
    where, width = const_columns()
    with ExitStack() as ctx:
        def sb(name, shape, dt=F32):
            return ctx.enter_context(nc.sbuf_tensor(f"w_{name}", shape, dt))

        w = {name: sb(name, shape) for name, shape in [
            ("const", [P, width]), ("early", [P, EARLY_WIDTH]), ("rows", [P, 5 * D]), ("late", [P, LATE_WIDTH]),
            ("w1", [P, E * DF]), ("w2", [P, E * DF]), ("b2", [P, E * D]), ("g2h", [P, D]), ("be2h", [P, D]),
            ("eps", [P, 1]), ("x", [P, NT * D]), ("res", [P, NT * D]), ("moments", [P, NT * 2]),
            ("moments1", [P, NT * 2]), ("logits", [P, NT * E])]}
        for whole, parts in [("early", EARLY_PARTS), ("rows", [(name, D) for name in ROWS]), ("late", LATE_PARTS)]:
            at = 0
            for name, columns in parts:
                w[name] = w[whole][:, at:at + columns]
                at += columns
        w["before16"], w["ones16"] = sb("before16", [P, P], BF16), sb("ones16", [P, P], BF16)
        for name in ["expert", "reads", "writes"]:
            w[name] = sb(name, [P, SLOTS], I32)
        w["values"] = [sb(f"values{b}", [P, H2 * HM]) for b in range(4)]
        c = {name: w["const"][:, a:b] for name, (a, b) in where.items()}
        dram["yx"] = nc.dram_tensor("rows_yx", [N, 2 * D], F32, kind="Internal").ap()
        dram["x1"] = nc.dram_tensor("rows_x1", [N + SPARE, D], F32, kind="Internal").ap()
        load_phase(nc, c, w, dram)
        attention_phase(nc, c, w, dram, "a1", [
            (w["w1"][:, :], dram["w1"]), (w["w2"][:, :], dram["w2"]), (w["late"][:, :], dram["late"]),
            (w["b2"][:, :], dram["b2"].rearrange("e d -> (e d)").partition_broadcast(P))])
        router_phase(nc, c, w, dram, "g1")
        routing_phase(nc, c, w, "r1")
        experts_phase(nc, c, w, dram, dram["x1"], "e1")
        linear_attention_phase(nc, c, w, dram["x1"], "la")
        attention_phase(nc, c, w, dram, "a2", [])
        router_phase(nc, c, w, dram, "g2")
        routing_phase(nc, c, w, "r2")
        experts_phase(nc, c, w, dram, out, "e2")


def shape_constants():
    import numpy as np
    where, width = const_columns()
    table = np.zeros((P, width), np.float32)

    def put(name, a):
        table[:, where[name][0]:where[name][1]] = a

    i = np.arange(P)
    put("ident", np.eye(P))
    put("upto", i[:, None] <= i[None, :])
    put("before", i[:, None] < i[None, :])
    put("later", i[:, None] > i[None, :])
    put("ones", 1.0)
    put("heads", i[:, None] // HD1 == np.arange(H1)[None, :])
    put("lane", i[None, :])
    put("slot", np.arange(SLOTS)[None, :])
    put("filled", (P * np.arange(NT))[None, :])
    put("rank", (E - np.arange(E))[None, :])
    put("part", i[:, None])
    put("spare", N + i[:, None] + P * np.arange(SLOTS)[None, :])
    g = np.arange(NT)
    put("high", ((g % S) * NJ + g // S)[None, :])
    power = np.power(np.float32(10000.0), np.arange(0, HD2, 2, dtype=np.float32) / np.float32(HD2))
    inv_freq = (np.float32(1.0) / power).astype(np.float32)
    freqs = np.arange(L, dtype=np.float32)[:, None] * inv_freq[None, :]
    cos = np.cos(freqs.astype(np.float64)).astype(np.float32)
    sin = np.sin(freqs.astype(np.float64)).astype(np.float32)
    cos2 = np.repeat(cos, 2, axis=1)
    sin2 = np.stack([-sin, sin], axis=2).reshape(L, HD2)
    put("cos", cos2.reshape(NJ, P, HD2).transpose(1, 0, 2).reshape(P, NJ * HD2))
    put("sin", sin2.reshape(NJ, P, HD2).transpose(1, 0, 2).reshape(P, NJ * HD2))
    return table


def kernel(**inputs):
    import numpy as np
    import concourse.bacc as bacc
    from concourse.bass_utils import run_bass_kernel_spmd

    def lay(name):
        return np.asarray(inputs[name])

    arrays = {
        "x": lay("L0_attn_x").reshape(N, D),
        "early": np.concatenate([lay("L0_ffn_Wqkv").T, lay("L0_ffn_Wo").T, lay("L0_ffn_Wg").T,
                                 lay("L0_ffn_bqkv").reshape(3, D).T], axis=1),
        "rows": np.concatenate([lay(f"L0_ffn_{name}") for name in ROWS]),
        "late": np.concatenate([lay("L0_attn_wq"), lay("L0_attn_wk"), lay("L0_attn_wv"), lay("L0_attn_wo"),
                                lay("L0_ffn_b1").reshape(E * NC, P).T], axis=1),
        "w1": lay("L0_ffn_W1").transpose(1, 0, 2).reshape(P, E * DF),
        "w2": lay("L0_ffn_W2").reshape(E, NC, P, D).transpose(2, 0, 1, 3).reshape(P, E * DF),
        "b2": lay("L0_ffn_b2"), "const": shape_constants(),
    }
    nc = bacc.Bacc("TRN2", target_bir_lowering=False, num_devices=1)
    sent, dram = {}, {}
    for name, a in arrays.items():
        sent[f"in_{name}"] = np.ascontiguousarray(a)
        dram[name] = nc.dram_tensor(f"in_{name}", list(a.shape), F32, kind="ExternalInput").ap()
    out = nc.dram_tensor("out", [N + SPARE, D], F32, kind="ExternalOutput").ap()
    macaron_kernel(nc, dram, out)
    r = run_bass_kernel_spmd(nc, [sent], core_ids=[0])
    return r.results[0]["out"][:N].reshape(S, L, D)
```
